# Optimizing a Trainium2 kernel written in Bass

```python
import numpy as np
import jax
import jax.numpy as jnp

def _softmax(x, axis=-1):
    return jax.nn.softmax(x, axis=axis)

def _gelu(x):
    return jax.nn.gelu(x, approximate=True)

def _silu(x):
    return jax.nn.silu(x)

def _sigmoid(x):
    return jax.nn.sigmoid(x)

def _layernorm(x, axis=-1, eps=1e-05):
    m = jnp.mean(x, axis=axis, keepdims=True)
    v = jnp.var(x, axis=axis, keepdims=True)
    return (x - m) / jnp.sqrt(v + eps)

def _scatter_add(tgt, idx, src, axis=0):
    return tgt.at[idx].add(src)

def _segment_sum(src, seg, n):
    return jax.ops.segment_sum(src, seg, n)
kernel_name = 'mk_xattn_seq_d4_seqx_r8_c029d6'

def setup_inputs(seed: int=0):
    np.random.seed(seed)
    _w = jnp.asarray

    def _rec_inputs():
        import jax
        import jax.numpy as jnp
        _rk = jax.random.key(seed)
        x = -0.0003929 + 0.9999 * jax.random.normal(jax.random.fold_in(_rk, 1), (2, 512, 128), jnp.float32)
        _lenS = 512 - jax.random.randint(jax.random.fold_in(_rk, 7), (2,), 0, max(1, 512 // 4) + 1, jnp.int32)
        _lenS2 = 32 - jax.random.randint(jax.random.fold_in(_rk, 8), (2,), 0, max(1, 32 // 4) + 1, jnp.int32)
        _ctx_512P = jax.random.normal(jax.random.fold_in(_rk, 11), (2, 16, 64), jnp.float32)
        _ctx_512c = jax.random.dirichlet(jax.random.fold_in(_rk, 511), 0.3 * jnp.ones((16,), jnp.float32), (2, 32))
        _ctx_512t = jnp.einsum('bsk,bkd->bsd', _ctx_512c, _ctx_512P)
        _ctx_512t = _ctx_512t * jax.lax.rsqrt(jnp.mean(jnp.square(_ctx_512t)) + 1e-12) * 0.953939
        ctx_512 = 4.13588e-05 + 0.999923 * (_ctx_512t + 0.3 * jax.random.normal(jax.random.fold_in(_rk, 611), (2, 32, 64), jnp.float32))
        _validS = jnp.arange(512)[None, :] < _lenS[:, None]
        _validS2 = jnp.arange(32)[None, :] < _lenS2[:, None]
        _causal = jnp.tril(jnp.ones((512, 512), dtype=bool))
        mask_BxSxS_ik0 = jnp.where(jnp.broadcast_to(_validS[:, None, :], (2, 512, 512)), 0, 1).astype(jnp.int32)
        mask_Bx1xS2_if1 = jnp.where(jnp.ones((2, 1, 32), dtype=bool), 1, 0).astype(jnp.int32)
        return (x, ctx_512, mask_BxSxS_ik0, mask_Bx1xS2_if1)
    x, ctx_512, mask_BxSxS_ik0, mask_Bx1xS2_if1 = _rec_inputs()

    def _L0_xattn_setup():
        import jax, jax.numpy as jnp
        import numpy as np
        QUERY_DIM = 128
        KEY_DIM = 64
        HIDDEN_DIM = 128
        B, LQ, LK = (8, 256, 256)
        key = jax.random.key(seed)
        ks = jax.random.split(key, 10)
        s_q = 1.0 / np.sqrt(QUERY_DIM)
        s_k = 1.0 / np.sqrt(KEY_DIM)
        s_h = 1.0 / np.sqrt(HIDDEN_DIM)
        return {'query': jax.random.normal(ks[0], (B, LQ, QUERY_DIM), jnp.float32), 'key': jax.random.normal(ks[1], (B, LK, KEY_DIM), jnp.float32), 'Wq': jax.random.uniform(ks[2], (QUERY_DIM, HIDDEN_DIM), jnp.float32, -s_q, s_q), 'bq': jax.random.uniform(ks[3], (HIDDEN_DIM,), jnp.float32, -s_q, s_q), 'Wk': jax.random.uniform(ks[4], (KEY_DIM, HIDDEN_DIM), jnp.float32, -s_k, s_k), 'bk': jax.random.uniform(ks[5], (HIDDEN_DIM,), jnp.float32, -s_k, s_k), 'Wv': jax.random.uniform(ks[6], (KEY_DIM, HIDDEN_DIM), jnp.float32, -s_k, s_k), 'bv': jax.random.uniform(ks[7], (HIDDEN_DIM,), jnp.float32, -s_k, s_k), 'Wo': jax.random.uniform(ks[8], (HIDDEN_DIM, QUERY_DIM), jnp.float32, -s_h, s_h), 'bo': jax.random.uniform(ks[9], (QUERY_DIM,), jnp.float32, -s_h, s_h)}
    _L0_xattn_all = _L0_xattn_setup()
    _L0_xattn_in = {k: v for k, v in _L0_xattn_all.items() if k in ('Wq', 'bq', 'Wk', 'bk', 'Wv', 'bv', 'Wo', 'bo')}
    del _L0_xattn_all

    def _L1_xattn_setup():
        import jax, jax.numpy as jnp
        import numpy as np
        B, ST, SS = (8, 64, 72)
        TD, SD = (128, 64)
        L, H, D, FF = (6, 16, 64, 512)

        def _ln(x, g, b, eps=1e-05):
            m = jnp.mean(x, axis=-1, keepdims=True)
            v = jnp.mean(jnp.square(x - m), axis=-1, keepdims=True)
            return (x - m) / jnp.sqrt(v + eps) * g + b

        def _heads(x):
            b, s, _ = x.shape
            return x.reshape(b, s, H, D).transpose(0, 2, 1, 3)

        def _mha(s, t, kv_w, q_w, o_w, o_b, mask):
            kv = s @ kv_w
            k, v = jnp.split(kv, 2, axis=-1)
            q = t @ q_w
            k, v, q = (_heads(k), _heads(v), _heads(q))
            scores = jnp.einsum('bhqd,bhkd->bhqk', q, k) * D ** (-0.5)
            scores = jnp.where(mask[:, None] == 0, jnp.float32(-1000000000.0), scores)
            attn = jax.nn.softmax(scores, axis=-1)
            o = jnp.einsum('bhqk,bhkd->bhqd', attn, v)
            o = o.transpose(0, 2, 1, 3).reshape(t.shape[0], t.shape[1], H * D)
            return o @ o_w + o_b
        key = jax.random.key(seed)
        ks = jax.random.split(key, 18)
        sc = 0.02
        inp = {'src': jax.random.normal(ks[0], (B, SS, SD), jnp.float32), 'tgt': jax.random.normal(ks[1], (B, ST, TD), jnp.float32), 'tgt_mask': jnp.broadcast_to(jnp.tril(jnp.ones((ST, ST), jnp.int32)), (B, ST, ST)), 'src_mask': jnp.ones((B, 1, SS), jnp.int32), 'norm_g': jnp.ones((TD,), jnp.float32), 'norm_b': jnp.zeros((TD,), jnp.float32), 'sa_kv': jax.random.normal(ks[2], (L, TD, 2 * H * D), jnp.float32) * sc, 'sa_q': jax.random.normal(ks[3], (L, TD, H * D), jnp.float32) * sc, 'sa_ow': jax.random.normal(ks[4], (L, H * D, TD), jnp.float32) * sc, 'sa_ob': jnp.zeros((L, TD), jnp.float32), 'ca_kv': jax.random.normal(ks[5], (L, SD, 2 * H * D), jnp.float32) * sc, 'ca_q': jax.random.normal(ks[6], (L, TD, H * D), jnp.float32) * sc, 'ca_ow': jax.random.normal(ks[7], (L, H * D, TD), jnp.float32) * sc, 'ca_ob': jnp.zeros((L, TD), jnp.float32), 'ff_w1': jax.random.normal(ks[8], (L, TD, FF), jnp.float32) * sc, 'ff_b1': jnp.zeros((L, FF), jnp.float32), 'ff_w2': jax.random.normal(ks[9], (L, FF, TD), jnp.float32) * sc, 'ff_b2': jnp.zeros((L, TD), jnp.float32), 'pre_g': jnp.ones((L, TD), jnp.float32), 'pre_b': jnp.zeros((L, TD), jnp.float32)}
        return inp
    _L1_xattn_all = _L1_xattn_setup()
    _L1_xattn_in = {k: v for k, v in _L1_xattn_all.items() if k in ('norm_g', 'norm_b', 'sa_kv', 'sa_q', 'sa_ow', 'sa_ob', 'ca_kv', 'ca_q', 'ca_ow', 'ca_ob', 'ff_w1', 'ff_b1', 'ff_w2', 'ff_b2', 'pre_g', 'pre_b')}
    del _L1_xattn_all

    def _L2_xattn_setup():
        import jax, jax.numpy as jnp
        import numpy as np
        B, T, E = (8, 512, 128)
        M, L = (32, 64)
        EPS = 1e-06
        key = jax.random.key(seed)
        ks = jax.random.split(key, 5)
        return {'emb': jax.random.normal(ks[0], (B, T, E), dtype=jnp.float32), 'latent': jax.random.normal(ks[1], (B, M, L), dtype=jnp.float32), 'Wq': jax.random.normal(ks[2], (E, E), dtype=jnp.float32) * (1.0 / np.sqrt(E)), 'bq': jnp.zeros((E,), dtype=jnp.float32), 'Wk': jax.random.normal(ks[3], (L, E), dtype=jnp.float32) * (1.0 / np.sqrt(L)), 'bk': jnp.zeros((E,), dtype=jnp.float32), 'Wv': jax.random.normal(ks[4], (L, E), dtype=jnp.float32) * (1.0 / np.sqrt(L)), 'bv': jnp.zeros((E,), dtype=jnp.float32), 'gamma': jnp.ones((E,), dtype=jnp.float32), 'beta': jnp.zeros((E,), dtype=jnp.float32)}
    _L2_xattn_all = _L2_xattn_setup()
    _L2_xattn_in = {k: v for k, v in _L2_xattn_all.items() if k in ('Wq', 'bq', 'Wk', 'bk', 'Wv', 'bv', 'gamma', 'beta')}
    del _L2_xattn_all

    def _L3_xattn_setup():
        import jax, jax.numpy as jnp
        import numpy as np
        B, ST, SS = (8, 64, 72)
        TD, SD = (128, 64)
        L, H, D, FF = (6, 16, 64, 512)

        def _ln(x, g, b, eps=1e-05):
            m = jnp.mean(x, axis=-1, keepdims=True)
            v = jnp.mean(jnp.square(x - m), axis=-1, keepdims=True)
            return (x - m) / jnp.sqrt(v + eps) * g + b

        def _heads(x):
            b, s, _ = x.shape
            return x.reshape(b, s, H, D).transpose(0, 2, 1, 3)

        def _mha(s, t, kv_w, q_w, o_w, o_b, mask):
            kv = s @ kv_w
            k, v = jnp.split(kv, 2, axis=-1)
            q = t @ q_w
            k, v, q = (_heads(k), _heads(v), _heads(q))
            scores = jnp.einsum('bhqd,bhkd->bhqk', q, k) * D ** (-0.5)
            scores = jnp.where(mask[:, None] == 0, jnp.float32(-1000000000.0), scores)
            attn = jax.nn.softmax(scores, axis=-1)
            o = jnp.einsum('bhqk,bhkd->bhqd', attn, v)
            o = o.transpose(0, 2, 1, 3).reshape(t.shape[0], t.shape[1], H * D)
            return o @ o_w + o_b
        key = jax.random.key(seed)
        ks = jax.random.split(key, 18)
        sc = 0.02
        inp = {'src': jax.random.normal(ks[0], (B, SS, SD), jnp.float32), 'tgt': jax.random.normal(ks[1], (B, ST, TD), jnp.float32), 'tgt_mask': jnp.broadcast_to(jnp.tril(jnp.ones((ST, ST), jnp.int32)), (B, ST, ST)), 'src_mask': jnp.ones((B, 1, SS), jnp.int32), 'norm_g': jnp.ones((TD,), jnp.float32), 'norm_b': jnp.zeros((TD,), jnp.float32), 'sa_kv': jax.random.normal(ks[2], (L, TD, 2 * H * D), jnp.float32) * sc, 'sa_q': jax.random.normal(ks[3], (L, TD, H * D), jnp.float32) * sc, 'sa_ow': jax.random.normal(ks[4], (L, H * D, TD), jnp.float32) * sc, 'sa_ob': jnp.zeros((L, TD), jnp.float32), 'ca_kv': jax.random.normal(ks[5], (L, SD, 2 * H * D), jnp.float32) * sc, 'ca_q': jax.random.normal(ks[6], (L, TD, H * D), jnp.float32) * sc, 'ca_ow': jax.random.normal(ks[7], (L, H * D, TD), jnp.float32) * sc, 'ca_ob': jnp.zeros((L, TD), jnp.float32), 'ff_w1': jax.random.normal(ks[8], (L, TD, FF), jnp.float32) * sc, 'ff_b1': jnp.zeros((L, FF), jnp.float32), 'ff_w2': jax.random.normal(ks[9], (L, FF, TD), jnp.float32) * sc, 'ff_b2': jnp.zeros((L, TD), jnp.float32), 'pre_g': jnp.ones((L, TD), jnp.float32), 'pre_b': jnp.zeros((L, TD), jnp.float32)}
        return inp
    _L3_xattn_all = _L3_xattn_setup()
    _L3_xattn_in = {k: v for k, v in _L3_xattn_all.items() if k in ('norm_g', 'norm_b', 'sa_kv', 'sa_q', 'sa_ow', 'sa_ob', 'ca_kv', 'ca_q', 'ca_ow', 'ca_ob', 'ff_w1', 'ff_b1', 'ff_w2', 'ff_b2', 'pre_g', 'pre_b')}
    del _L3_xattn_all
    return {'x': x, 'ctx_512': ctx_512, 'mask_BxSxS_ik0': mask_BxSxS_ik0, 'mask_Bx1xS2_if1': mask_Bx1xS2_if1, 'L0_xattn_Wq': _L0_xattn_in['Wq'], 'L0_xattn_bq': _L0_xattn_in['bq'], 'L0_xattn_Wk': _L0_xattn_in['Wk'], 'L0_xattn_bk': _L0_xattn_in['bk'], 'L0_xattn_Wv': _L0_xattn_in['Wv'], 'L0_xattn_bv': _L0_xattn_in['bv'], 'L0_xattn_Wo': _L0_xattn_in['Wo'], 'L0_xattn_bo': _L0_xattn_in['bo'], 'L1_xattn_norm_g': _L1_xattn_in['norm_g'], 'L1_xattn_norm_b': _L1_xattn_in['norm_b'], 'L1_xattn_sa_kv': _L1_xattn_in['sa_kv'], 'L1_xattn_sa_q': _L1_xattn_in['sa_q'], 'L1_xattn_sa_ow': _L1_xattn_in['sa_ow'], 'L1_xattn_sa_ob': _L1_xattn_in['sa_ob'], 'L1_xattn_ca_kv': _L1_xattn_in['ca_kv'], 'L1_xattn_ca_q': _L1_xattn_in['ca_q'], 'L1_xattn_ca_ow': _L1_xattn_in['ca_ow'], 'L1_xattn_ca_ob': _L1_xattn_in['ca_ob'], 'L1_xattn_ff_w1': _L1_xattn_in['ff_w1'], 'L1_xattn_ff_b1': _L1_xattn_in['ff_b1'], 'L1_xattn_ff_w2': _L1_xattn_in['ff_w2'], 'L1_xattn_ff_b2': _L1_xattn_in['ff_b2'], 'L1_xattn_pre_g': _L1_xattn_in['pre_g'], 'L1_xattn_pre_b': _L1_xattn_in['pre_b'], 'L2_xattn_Wq': _L2_xattn_in['Wq'], 'L2_xattn_bq': _L2_xattn_in['bq'], 'L2_xattn_Wk': _L2_xattn_in['Wk'], 'L2_xattn_bk': _L2_xattn_in['bk'], 'L2_xattn_Wv': _L2_xattn_in['Wv'], 'L2_xattn_bv': _L2_xattn_in['bv'], 'L2_xattn_gamma': _L2_xattn_in['gamma'], 'L2_xattn_beta': _L2_xattn_in['beta'], 'L3_xattn_norm_g': _L3_xattn_in['norm_g'], 'L3_xattn_norm_b': _L3_xattn_in['norm_b'], 'L3_xattn_sa_kv': _L3_xattn_in['sa_kv'], 'L3_xattn_sa_q': _L3_xattn_in['sa_q'], 'L3_xattn_sa_ow': _L3_xattn_in['sa_ow'], 'L3_xattn_sa_ob': _L3_xattn_in['sa_ob'], 'L3_xattn_ca_kv': _L3_xattn_in['ca_kv'], 'L3_xattn_ca_q': _L3_xattn_in['ca_q'], 'L3_xattn_ca_ow': _L3_xattn_in['ca_ow'], 'L3_xattn_ca_ob': _L3_xattn_in['ca_ob'], 'L3_xattn_ff_w1': _L3_xattn_in['ff_w1'], 'L3_xattn_ff_b1': _L3_xattn_in['ff_b1'], 'L3_xattn_ff_w2': _L3_xattn_in['ff_w2'], 'L3_xattn_ff_b2': _L3_xattn_in['ff_b2'], 'L3_xattn_pre_g': _L3_xattn_in['pre_g'], 'L3_xattn_pre_b': _L3_xattn_in['pre_b']}

def reference(x, ctx_512, mask_BxSxS_ik0, mask_Bx1xS2_if1, L0_xattn_Wq, L0_xattn_bq, L0_xattn_Wk, L0_xattn_bk, L0_xattn_Wv, L0_xattn_bv, L0_xattn_Wo, L0_xattn_bo, L1_xattn_norm_g, L1_xattn_norm_b, L1_xattn_sa_kv, L1_xattn_sa_q, L1_xattn_sa_ow, L1_xattn_sa_ob, L1_xattn_ca_kv, L1_xattn_ca_q, L1_xattn_ca_ow, L1_xattn_ca_ob, L1_xattn_ff_w1, L1_xattn_ff_b1, L1_xattn_ff_w2, L1_xattn_ff_b2, L1_xattn_pre_g, L1_xattn_pre_b, L2_xattn_Wq, L2_xattn_bq, L2_xattn_Wk, L2_xattn_bk, L2_xattn_Wv, L2_xattn_bv, L2_xattn_gamma, L2_xattn_beta, L3_xattn_norm_g, L3_xattn_norm_b, L3_xattn_sa_kv, L3_xattn_sa_q, L3_xattn_sa_ow, L3_xattn_sa_ob, L3_xattn_ca_kv, L3_xattn_ca_q, L3_xattn_ca_ow, L3_xattn_ca_ob, L3_xattn_ff_w1, L3_xattn_ff_b1, L3_xattn_ff_w2, L3_xattn_ff_b2, L3_xattn_pre_g, L3_xattn_pre_b):
    import jax
    import jax.numpy as jnp

    def _L0_xattn_ref(query, key, Wq, bq, Wk, bk, Wv, bv, Wo, bo):
        import jax, jax.numpy as jnp
        import numpy as np
        QUERY_DIM = 128
        KEY_DIM = 64
        HIDDEN_DIM = 128
        B, LQ, LK = (8, 256, 256)
        scale = HIDDEN_DIM ** (-0.5)
        Q = jnp.einsum('bqd,dh->bqh', query, Wq) + bq
        K = jnp.einsum('bkd,dh->bkh', key, Wk) + bk
        V = jnp.einsum('bkd,dh->bkh', key, Wv) + bv
        scores = jnp.einsum('bqh,bkh->bqk', Q, K) * scale
        weights = jax.nn.softmax(scores, axis=-1)
        attended = jnp.einsum('bqk,bkh->bqh', weights, V)
        out = jnp.einsum('bqh,hd->bqd', attended, Wo) + bo
        return query + out

    def _L1_xattn_ref(src, tgt, tgt_mask, src_mask, norm_g, norm_b, sa_kv, sa_q, sa_ow, sa_ob, ca_kv, ca_q, ca_ow, ca_ob, ff_w1, ff_b1, ff_w2, ff_b2, pre_g, pre_b):
        import jax, jax.numpy as jnp
        import numpy as np
        B, ST, SS = (8, 64, 72)
        TD, SD = (128, 64)
        L, H, D, FF = (6, 16, 64, 512)

        def _ln(x, g, b, eps=1e-05):
            m = jnp.mean(x, axis=-1, keepdims=True)
            v = jnp.mean(jnp.square(x - m), axis=-1, keepdims=True)
            return (x - m) / jnp.sqrt(v + eps) * g + b

        def _heads(x):
            b, s, _ = x.shape
            return x.reshape(b, s, H, D).transpose(0, 2, 1, 3)

        def _mha(s, t, kv_w, q_w, o_w, o_b, mask):
            kv = s @ kv_w
            k, v = jnp.split(kv, 2, axis=-1)
            q = t @ q_w
            k, v, q = (_heads(k), _heads(v), _heads(q))
            scores = jnp.einsum('bhqd,bhkd->bhqk', q, k) * D ** (-0.5)
            scores = jnp.where(mask[:, None] == 0, jnp.float32(-1000000000.0), scores)
            attn = jax.nn.softmax(scores, axis=-1)
            o = jnp.einsum('bhqk,bhkd->bhqd', attn, v)
            o = o.transpose(0, 2, 1, 3).reshape(t.shape[0], t.shape[1], H * D)
            return o @ o_w + o_b
        stacked = (sa_kv, sa_q, sa_ow, sa_ob, ca_kv, ca_q, ca_ow, ca_ob, ff_w1, ff_b1, ff_w2, ff_b2, pre_g, pre_b)

        def step(t, p):
            skv, sq, sow, sob, ckv, cq, cow, cob, w1, b1, w2, b2, pg, pb = p
            tn = _ln(t, norm_g, norm_b)
            t = _mha(tn, tn, skv, sq, sow, sob, tgt_mask) + t
            tn = _ln(t, norm_g, norm_b)
            t = _mha(src, tn, ckv, cq, cow, cob, src_mask) + t
            tn = _ln(t, pg, pb)
            t = t + (jax.nn.relu(tn @ w1 + b1) @ w2 + b2)
            return (t, None)
        out, _ = jax.lax.scan(step, tgt, stacked)
        return out

    def _L2_xattn_ref(emb, latent, Wq, bq, Wk, bk, Wv, bv, gamma, beta):
        import jax, jax.numpy as jnp
        import numpy as np
        B, T, E = (8, 512, 128)
        M, L = (32, 64)
        EPS = 1e-06
        q = jnp.einsum('bte,ef->btf', emb, Wq) + bq
        k = jnp.einsum('bml,le->bme', latent, Wk) + bk
        v = jnp.einsum('bml,le->bme', latent, Wv) + bv
        scale = 1.0 / jnp.sqrt(jnp.asarray(E, dtype=q.dtype))
        w = jnp.einsum('bte,bme->btm', q, k) * scale
        w = jax.nn.softmax(w, axis=1)
        pred = jnp.einsum('btm,bme->bte', w, v)
        x = pred + emb
        mu = jnp.mean(x, axis=-1, keepdims=True)
        var = jnp.var(x, axis=-1, keepdims=True)
        return (x - mu) * jax.lax.rsqrt(var + EPS) * gamma + beta

    def _L3_xattn_ref(src, tgt, tgt_mask, src_mask, norm_g, norm_b, sa_kv, sa_q, sa_ow, sa_ob, ca_kv, ca_q, ca_ow, ca_ob, ff_w1, ff_b1, ff_w2, ff_b2, pre_g, pre_b):
        import jax, jax.numpy as jnp
        import numpy as np
        B, ST, SS = (8, 64, 72)
        TD, SD = (128, 64)
        L, H, D, FF = (6, 16, 64, 512)

        def _ln(x, g, b, eps=1e-05):
            m = jnp.mean(x, axis=-1, keepdims=True)
            v = jnp.mean(jnp.square(x - m), axis=-1, keepdims=True)
            return (x - m) / jnp.sqrt(v + eps) * g + b

        def _heads(x):
            b, s, _ = x.shape
            return x.reshape(b, s, H, D).transpose(0, 2, 1, 3)

        def _mha(s, t, kv_w, q_w, o_w, o_b, mask):
            kv = s @ kv_w
            k, v = jnp.split(kv, 2, axis=-1)
            q = t @ q_w
            k, v, q = (_heads(k), _heads(v), _heads(q))
            scores = jnp.einsum('bhqd,bhkd->bhqk', q, k) * D ** (-0.5)
            scores = jnp.where(mask[:, None] == 0, jnp.float32(-1000000000.0), scores)
            attn = jax.nn.softmax(scores, axis=-1)
            o = jnp.einsum('bhqk,bhkd->bhqd', attn, v)
            o = o.transpose(0, 2, 1, 3).reshape(t.shape[0], t.shape[1], H * D)
            return o @ o_w + o_b
        stacked = (sa_kv, sa_q, sa_ow, sa_ob, ca_kv, ca_q, ca_ow, ca_ob, ff_w1, ff_b1, ff_w2, ff_b2, pre_g, pre_b)

        def step(t, p):
            skv, sq, sow, sob, ckv, cq, cow, cob, w1, b1, w2, b2, pg, pb = p
            tn = _ln(t, norm_g, norm_b)
            t = _mha(tn, tn, skv, sq, sow, sob, tgt_mask) + t
            tn = _ln(t, norm_g, norm_b)
            t = _mha(src, tn, ckv, cq, cow, cob, src_mask) + t
            tn = _ln(t, pg, pb)
            t = t + (jax.nn.relu(tn @ w1 + b1) @ w2 + b2)
            return (t, None)
        out, _ = jax.lax.scan(step, tgt, stacked)
        return out
    x = _L0_xattn_ref(x, ctx_512, L0_xattn_Wq, L0_xattn_bq, L0_xattn_Wk, L0_xattn_bk, L0_xattn_Wv, L0_xattn_bv, L0_xattn_Wo, L0_xattn_bo)
    x = _L1_xattn_ref(ctx_512, x, mask_BxSxS_ik0, mask_Bx1xS2_if1, L1_xattn_norm_g, L1_xattn_norm_b, L1_xattn_sa_kv, L1_xattn_sa_q, L1_xattn_sa_ow, L1_xattn_sa_ob, L1_xattn_ca_kv, L1_xattn_ca_q, L1_xattn_ca_ow, L1_xattn_ca_ob, L1_xattn_ff_w1, L1_xattn_ff_b1, L1_xattn_ff_w2, L1_xattn_ff_b2, L1_xattn_pre_g, L1_xattn_pre_b)
    x = _L2_xattn_ref(x, ctx_512, L2_xattn_Wq, L2_xattn_bq, L2_xattn_Wk, L2_xattn_bk, L2_xattn_Wv, L2_xattn_bv, L2_xattn_gamma, L2_xattn_beta)
    x = _L3_xattn_ref(ctx_512, x, mask_BxSxS_ik0, mask_Bx1xS2_if1, L3_xattn_norm_g, L3_xattn_norm_b, L3_xattn_sa_kv, L3_xattn_sa_q, L3_xattn_sa_ow, L3_xattn_sa_ob, L3_xattn_ca_kv, L3_xattn_ca_q, L3_xattn_ca_ow, L3_xattn_ca_ob, L3_xattn_ff_w1, L3_xattn_ff_b1, L3_xattn_ff_w2, L3_xattn_ff_b2, L3_xattn_pre_g, L3_xattn_pre_b)
    return x

_drawn_inputs = setup_inputs


def setup_inputs(seed=0):
    import zlib

    import numpy as np

    out = dict(_drawn_inputs(seed))
    spreads = {'L1_xattn_norm_g': (1.0, 0.6),
     'L1_xattn_norm_b': (0.0, 0.1),
     'L1_xattn_sa_ob': (0.0, 0.1),
     'L1_xattn_ca_ob': (0.0, 0.1),
     'L1_xattn_ff_b1': (0.0, 0.1),
     'L1_xattn_ff_b2': (0.0, 0.1),
     'L1_xattn_pre_g': (1.0, 0.572),
     'L1_xattn_pre_b': (0.0, 0.55),
     'L2_xattn_bq': (0.0, 2.0),
     'L2_xattn_bk': (0.0, 0.8),
     'L2_xattn_bv': (0.0, 0.8),
     'L2_xattn_gamma': (1.0, 0.2),
     'L2_xattn_beta': (0.0, 0.1),
     'L3_xattn_norm_g': (1.0, 0.2),
     'L3_xattn_norm_b': (0.0, 0.1),
     'L3_xattn_sa_ob': (0.0, 0.1),
     'L3_xattn_ca_ob': (0.0, 0.1),
     'L3_xattn_ff_b1': (0.0, 0.1),
     'L3_xattn_ff_b2': (0.0, 0.1),
     'L3_xattn_pre_g': (1.0, 0.578),
     'L3_xattn_pre_b': (0.0, 0.535)}
    factors = {'L0_xattn_Wq': 3.131,
     'L0_xattn_bq': 8.0,
     'L0_xattn_Wk': 3.149,
     'L0_xattn_bk': 64.0,
     'L1_xattn_sa_q': 8.0,
     'L1_xattn_ca_q': 24.873,
     'L3_xattn_sa_q': 29.527,
     'L3_xattn_ca_q': 31.766}
    for name, (base, spread) in spreads.items():
        noise = np.random.default_rng([zlib.crc32(name.encode()), seed]).standard_normal(out[name].shape)
        drawn = base * np.exp(spread * noise) if base else spread * noise
        out[name] = jnp.asarray(drawn.astype(out[name].dtype))
    for name, factor in factors.items():
        out[name] = (out[name] * factor).astype(out[name].dtype)
    return out
```

```python
from contextlib import ExitStack

import concourse.bass as bass
from concourse import mybir

F32 = mybir.dt.float32
F32R = mybir.dt.float32r
BF16 = mybir.dt.bfloat16
I32 = mybir.dt.int32
ALU = mybir.AluOpType
ACT = mybir.ActivationFunctionType
AX = mybir.AxisListType

B = 2
S = 512
D = 128
SK = 32
DK = 64
H = 16
HD = 64
NP = H // 2
FF = 512
NL = 6
QT = S // 128
NT = B * QT
KT = S // 128
NF = FF // 128
SCALE = HD ** -0.5
MASKED = -1.0e30
SCALE1 = 128 ** -0.5
EPS = 1e-5
EPS2 = 1e-6

FREE = 1

FILLS = 9 * NP
SPLITS = 5 * NP


def build(nc, x, ctx, mask, cmask, w0, w0kv, w2, w2kv, rows0, rows2, cols0, cols2, wqk, wv, wo, ckv, cqo, ffw, cols, rows,
          norms, out):
    st = ExitStack()
    with st:
        def sb(name, shape, dt=F32):
            return st.enter_context(nc.sbuf_tensor(name, shape, dt))

        def sem(name):
            return st.enter_context(nc.semaphore(name))

        t = sb("t", [128, NT, D])
        cap = sb("cap", [128, NT, S])
        ccap = sb("ccap", [128, B, SK])
        ident = sb("ident", [128, 128])
        zeros = sb("zeros", [128, S], BF16)
        neghalf = sb("neghalf", [128, NT])
        ctx_sb = sb("ctx_sb", [B * SK, DK])
        ctxT = sb("ctxT", [DK, B * SK])
        norm_sb = sb("norm_sb", [128, 2, 2])
        stats = sb("stats", [128, NT, 6])
        mv = sb("mv", [128, NT, 2])
        vpe = sb("vpe", [128, NT])
        rstd = sb("rstd", [128, NT])
        xhat = sb("xhat", [128, NT, D])
        tnT = sb("tnT", [128, B, S])
        tnh = sb("tnh", [128, B, S], F32R)
        tnl = sb("tnl", [128, B, S], F32R)
        wqk_sb = sb("wqk_sb", [HD, 2, 2, D])
        wv_sb = sb("wv_sb", [128, 128])
        wo_sb = sb("wo_sb", [128, D])
        Ah = sb("Ah", [128, 2, D], F32R)
        Al = sb("Al", [128, 2, D], F32R)
        Hh = sb("Hh", [128, B, 2, S], F32R)
        Hl = sb("Hl", [128, B, 2, S], F32R)
        V = sb("V", [128, NT, 128])
        Ms = sb("Ms", [128, 2, 2, S])
        nmax = sb("nmax", [128, 2, 2])
        E = sb("E", [128, 2, 2, S])
        rsum = sb("rsum", [128, B, 2, QT])
        rinv = sb("rinv", [128, B, 2, QT])
        rx = sb("rx", [128, QT, 2, HD])
        PT = sb("PT", [128, 2, 2, KT, 128])
        Rsb = sb("Rsb", [128, S])
        OT = sb("OT", [128, S])
        ckv_sb = sb("ckv_sb", [DK, 2, NP, 128])
        cqo_sb = sb("cqo_sb", [128, 2, NP, D])
        KBD = sb("KBD", [128, NP, B, 2, SK])
        VBD = sb("VBD", [128, NP, B, 2, SK])
        Mw = sb("Mw", [128, B, H * SK])
        Nw = sb("Nw", [128, B, 4, D])
        XB = sb("XB", [128, 4, H, SK])
        xmax = sb("xmax", [128, 2, H])
        xsum = sb("xsum", [128, 2, H])
        xinv = sb("xinv", [128, 2, H])
        PX = sb("PX", [128, 2, 4, 128])
        ffw_sb = sb("ffw_sb", [128, 2, FF])
        cols_sb = sb("cols_sb", [128, 2 + NF])
        rows_sb = sb("rows_sb", [128, 3, D])
        hT = sb("hT", [128, NF, B, S])
        m_sb = sb("m_sb", [128, NT, S], I32)
        cm_sb = sb("cm_sb", [128, B, SK], I32)
        w0_sb = sb("w0_sb", [128, 2, 128])
        w0kv_sb = sb("w0kv_sb", [DK, 2, 128])
        w2_sb = sb("w2_sb", [128, 1, 128])
        w2kv_sb = sb("w2kv_sb", [DK, 2, 128])
        rows0_sb = sb("rows0_sb", [128, 2, D])
        rows2_sb = sb("rows2_sb", [128, 3, D])
        cols0_sb = sb("cols0_sb", [128, 2])
        cols2_sb = sb("cols2_sb", [128, 2])
        xT = sb("xT", [128, B, S])
        q0T = sb("q0T", [128, B, S])
        k0T = sb("k0T", [128, B * SK])
        v0 = sb("v0", [B * SK, D])
        v2 = sb("v2", [B * SK, B, D])
        s0 = sb("s0", [128, NT, SK])
        p0 = sb("p0", [128, NT, B * SK])
        m0 = sb("m0", [128, NT])
        z0 = sb("z0", [128, NT])
        p0T = sb("p0T", [B * SK, B, S])
        a0T = sb("a0T", [128, B, S])
        p2 = sb("p2", [B * SK, S])
        m2 = sb("m2", [B * SK, 1])
        z2 = sb("z2", [B * SK, 1])

        SC = [st.enter_context(nc.psum_tensor(f"SC{h}", [128, S], F32)) for h in range(2)]
        TR = [st.enter_context(nc.psum_tensor(f"TR{h}", [128, 4, 128], F32)) for h in range(2)]
        O = st.enter_context(nc.psum_tensor("O", [128, S], F32))
        X = st.enter_context(nc.psum_tensor("X", [128, S], F32))
        ACC = [st.enter_context(nc.psum_tensor(f"ACC{b}", [128, QT, D], F32)) for b in range(B)]

        ld_in = sem("ld_in")
        ld_w0 = sem("ld_w0")
        const_ready = sem("const_ready")
        cap_ready = sem("cap_ready")
        bd_zero = sem("bd_zero")
        pe1 = sem("pe1_products")
        dve1 = sem("dve1_stages")
        act1 = sem("act1_stages")
        res_ready = sem("res_ready")
        ln_stats = sem("ln_stats")
        ln_mv = sem("ln_mv")
        ln_vpe = sem("ln_vpe")
        ln_rstd = sem("ln_rstd")
        ln_xhat = sem("ln_xhat")
        ln_xhatT = sem("ln_xhatT")
        tn_dve = sem("tn_dve")
        tn_act = sem("tn_act")
        bias_added = sem("bias_added")
        acc_ready = sem("acc_ready")
        ld_wqk = sem("ld_wqk")
        ld_wv = sem("ld_wv")
        ld_wo = sem("ld_wo")
        ld_ckv = sem("ld_ckv")
        ld_cqo = sem("ld_cqo")
        ld_ff = sem("ld_ff")
        wo_used = sem("wo_used")
        fill = sem("spare_filled")
        fill_read = sem("spare_read")
        split_hi = sem("split_hi")
        scored = [sem(f"scored{h}") for h in range(2)]
        capped = [sem(f"capped{h}") for h in range(2)]
        expd = [sem(f"expd{h}") for h in range(2)]
        turned = [sem(f"turned{h}") for h in range(2)]
        pt_ready = [sem(f"pt_ready{h}") for h in range(2)]
        pv_done = sem("pv_done")
        rinv_ready = sem("rinv_ready")
        rx_ready = sem("rx_ready")
        ot_ready = sem("ot_ready")
        c_kv = sem("c_kv")
        c_bd = sem("c_bd")
        c_mn = sem("c_mn")
        c_mn_sb = sem("c_mn_sb")
        x_scored = sem("x_scored")
        x_capped = sem("x_capped")
        x_max = sem("x_max")
        x_sub = sem("x_sub")
        x_exp = sem("x_exp")
        x_sum = sem("x_sum")
        x_inv = sem("x_inv")
        x_norm = sem("x_norm")
        x_turned = sem("x_turned")
        x_pt = sem("x_pt")
        x_out = sem("x_out")
        ff_h = sem("ff_h")
        ff_relu = [sem("ff_relu_act"), sem("ff_relu_dve")]
        dve_passed = sem("dve_passed")
        pool_passed = sem("pool_passed")
        stored = sem("stored")

        block = st.enter_context(nc.Block())

        TND, TNA = 6, 4

        @block.sync
        def _(sp):
            for free in (fill, wo_used, c_mn):
                sp.sem_inc(free, FREE)
            sp.dma_start(t[:, :, :], x.rearrange("b (q p) d -> p (b q) d", p=128)).then_inc(ld_in, 16)
            sp.dma_start(ctx_sb[:, :], ctx.rearrange("b m d -> (b m) d")).then_inc(ld_in, 16)
            sp.dma_start(w0_sb[:, :, :], w0).then_inc(ld_w0, 16)
            sp.dma_start(w2_sb[:, :, :], w2).then_inc(ld_w0, 16)
            sp.dma_start(w0kv_sb[:, :, :], w0kv).then_inc(ld_w0, 16)
            sp.dma_start(w2kv_sb[:, :, :], w2kv).then_inc(ld_w0, 16)
            sp.dma_start(cols0_sb[:, :], cols0).then_inc(ld_w0, 16)
            sp.dma_start(cols2_sb[:, :], cols2).then_inc(ld_w0, 16)
            sp.dma_start(rows0_sb[:, :, :], rows0.partition_broadcast(128)).then_inc(ld_w0, 16)
            sp.dma_start(rows2_sb[:, :, :], rows2.partition_broadcast(128)).then_inc(ld_w0, 16)
            sp.dma_start(norm_sb[:, :, :], norms).then_inc(ld_w0, 16)
            sp.dma_start(cm_sb[:, :, :], cmask.rearrange("b o m -> (b o) m").partition_broadcast(128)).then_inc(ld_in, 16)
            sp.dma_start(m_sb[:, :, :], mask.rearrange("b (q p) k -> p (b q) k", p=128)).then_inc(ld_in, 16)

            def pair_weights(it, folded, valued):
                sp.wait_ge(fill, FREE + folded)
                sp.dma_start(wqk_sb[:, :, :, :],
                             wqk[bass.ds(it, 1), :, :, :, :].rearrange("o p a h n -> (o p) a h n")).then_inc(ld_wqk, 16)
                sp.wait_ge(fill, FREE + valued)
                sp.dma_start(wv_sb[:, :], wv[bass.ds(it, 1), :, :].rearrange("o p n -> (o p) n")).then_inc(ld_wv, 16)
                sp.wait_ge(wo_used, FREE + it)
                sp.dma_start(wo_sb[:, :], wo[bass.ds(it, 1), :, :].rearrange("o p n -> (o p) n")).then_inc(ld_wo, 16)

            for k in range(2):
                with sp.Fori(0, NL) as l:
                    g = l + k * NL
                    pair_weights(g * NP, g * FILLS, g * FILLS)
                    sp.wait_ge(c_mn, FREE + g * 2)
                    sp.dma_start(ckv_sb[:, :, :, :], ckv[bass.ds(g, 1), :, :, :, :].rearrange("o p a n d -> (o p) a n d")).then_inc(ld_ckv, 16)
                    sp.dma_start(cqo_sb[:, :, :, :], cqo[bass.ds(g, 1), :, :, :, :].rearrange("o p a n d -> (o p) a n d")).then_inc(ld_cqo, 16)
                    sp.wait_ge(res_ready, (g * 3 + k) * 2 + 2)
                    sp.dma_start(ffw_sb[:, :, :], ffw[bass.ds(g, 1), :, :, :].rearrange("o p a n -> (o p) a n")).then_inc(ld_ff, 16)
                    sp.dma_start(cols_sb[:, :], cols[bass.ds(g, 1), :, :].rearrange("o p n -> (o p) n")).then_inc(ld_ff, 16)
                    sp.dma_start(rows_sb[:, :, :], rows[bass.ds(g, 1), :, :].rearrange("o a n -> (o a) n").partition_broadcast(128)).then_inc(ld_ff, 16)
                    with sp.Fori(1, NP) as p:
                        pair_weights(g * NP + p, g * FILLS + p * 9 - 5, g * FILLS + p * 9 - 4)
            sp.wait_ge(res_ready, 2 + 2 * 3 * NL * 2 + 2)
            sp.dma_start(out.rearrange("b (q p) d -> p (b q) d", p=128), t[:, :, :]).then_inc(stored, 16)
            sp.wait_ge(stored, 16)

        @block.gpsimd
        def _(pool):
            pool.memset(ident[:, :], 0.0).then_inc(const_ready, 1)
            pool.wait_ge(const_ready, 1)
            pool.affine_select(out=ident[:, :], in_=ident[:, :], compare_op=ALU.not_equal, fill=1.0,
                               base=0, pattern=[[-1, 128]], channel_multiplier=1).then_inc(const_ready, 1)
            pool.memset(zeros[:, :], 0.0).then_inc(const_ready, 1)
            pool.memset(neghalf[:, :], -0.5).then_inc(const_ready, 1)
            pool.memset(p0[:, :, :], 0.0).then_inc(bd_zero, 1)
            pool.memset(v2[:, :, :], 0.0).then_inc(bd_zero, 1)
            pool.memset(KBD[:, :, :, :, :], 0.0).then_inc(bd_zero, 1)
            pool.memset(VBD[:, :, :, :, :], 0.0).then_inc(bd_zero, 1)

            def norm_factor(i, eps):
                pool.wait_ge(ln_mv, (i + 1) * NT)
                pool.sem_inc(pool_passed, 1)
                pool.tensor_scalar(vpe[:, :], mv[:, :, 1:2].rearrange("p j o -> p (j o)"), eps, None,
                                   ALU.add).then_inc(ln_vpe, 1)
                pool.wait_ge(ln_vpe, i + 1)
                pool.tensor_tensor(rstd[:, :], vpe[:, :], neghalf[:, :], ALU.pow).then_inc(ln_rstd, 1)

            def add_bias(i, sub):
                pool.wait_ge(ln_xhat, (i + 1) * NT)
                for b in range(B):
                    pool.tensor_tensor(t[:, QT * b:QT * b + QT, :], t[:, QT * b:QT * b + QT, :],
                                       rows_sb[:, sub:sub + 1, :].to_broadcast([128, QT, D]),
                                       ALU.add).then_inc(bias_added, 1)

            def spread_sums(it):
                for b in range(B):
                    pool.wait_ge(rinv_ready, it * 2 + b + 1)
                    pool.sem_inc(pool_passed, 1)
                    pool.tensor_copy(rx[:, :, :, :], rinv[:, b, :, :].rearrange("p h q -> p q h").unsqueeze(3)
                                     .to_broadcast([128, QT, 2, HD])).then_inc(rx_ready, 1)

            def cross_norm(n, j):
                pool.wait_ge(x_inv, n + 1)
                pool.tensor_tensor(XB[:, j % 4, :, :], XB[:, j % 4, :, :],
                                   xinv[:, j % 2, :].unsqueeze(2).to_broadcast([128, H, SK]),
                                   ALU.mult).then_inc(x_norm, 1)

            for k in range(2):
                if k:
                    norm_factor(3 * NL, EPS2)
                with pool.Fori(0, NL) as l:
                    g = l + k * NL
                    i = g * 3 + k
                    norm_factor(i, EPS)
                    pool.wait_ge(ld_ff, (g + 1) * 48)
                    add_bias(i, 0)
                    with pool.Fori(0, NP) as p:
                        spread_sums(g * NP + p)
                    norm_factor(i + 1, EPS)
                    add_bias(i + 1, 1)
                    for j in range(NT):
                        pool.wait_ge(x_max, g * NT + j + 1)
                        pool.tensor_tensor(XB[:, j % 4, :, :], XB[:, j % 4, :, :],
                                           xmax[:, j % 2, :].unsqueeze(2).to_broadcast([128, H, SK]),
                                           ALU.subtract).then_inc(x_sub, 1)
                        if j >= 1:
                            cross_norm(g * NT + j - 1, j - 1)
                    cross_norm(g * NT + NT - 1, NT - 1)
                    norm_factor(i + 2, EPS)
                    add_bias(i + 2, 2)

        @block.vector
        def _(dve):
            dve.wait_ge(ld_in, 64)
            dve.tensor_scalar(ccap[:, :, :], cm_sb[:, :, :], 0, MASKED, ALU.is_equal, ALU.mult).then_inc(cap_ready, 1)
            dve.tensor_scalar(cap[:, :, :], m_sb[:, :, :], 0, MASKED, ALU.is_equal, ALU.mult).then_inc(cap_ready, 1)
            dve.wait_ge(cap_ready, 2)

            n1 = 0

            def stage1(ins):
                nonlocal n1
                n1 += 1
                ins.then_inc(dve1, 1)

            def read_T(dst, cols_src=None):
                for b in range(B):
                    stage1(dve.tensor_copy(dst[:, b, :], TR[b][:, :, :].rearrange("p q d -> p (q d)")))

            def queries_keys_values(cols_sb_, rows_, v_stage):
                for b in range(B):
                    stage1(dve.tensor_scalar(q0T[:, b, :], SC[b][:, :], cols_sb_[:, 0:1], None, ALU.add))
                stage1(dve.tensor_scalar(k0T[:, :], X[:, 0:B * SK], cols_sb_[:, 1:2], None, ALU.add))
                v_stage()

            dve.wait_ge(pe1, 1)
            stage1(dve.tensor_copy(ctxT[:, :], X[0:DK, 0:B * SK]))
            read_T(xT)
            dve.wait_ge(pe1, 2)
            dve.wait_ge(ld_w0, 144)
            queries_keys_values(cols0_sb, rows0_sb, lambda: stage1(
                dve.tensor_tensor(v0[:, :], O[0:B * SK, 0:D], rows0_sb[0:B * SK, 0, :], ALU.add)))
            dve.wait_ge(pe1, 3)
            scores0 = X[:, 0:NT * SK].rearrange("p (j m) -> p j m", j=NT)
            stage1(dve.tensor_reduce(m0[:, :], scores0, AX.X, ALU.max))
            dve.wait_ge(dve1, 8)
            stage1(dve.tensor_tensor(s0[:, :, :], scores0,
                                     m0[:, :].unsqueeze(2).to_broadcast([128, NT, SK]), ALU.subtract))
            dve.wait_ge(act1, 1)
            stage1(dve.tensor_reduce(z0[:, :], s0[:, :, :], AX.X, ALU.add))
            dve.wait_ge(dve1, 10)
            stage1(dve.reciprocal(m0[:, :], z0[:, :]))
            dve.wait_ge(dve1, 11)
            dve.wait_ge(bd_zero, 4)
            for b in range(B):
                stage1(dve.tensor_tensor(p0[:, QT * b:QT * b + QT, SK * b:SK * b + SK], s0[:, QT * b:QT * b + QT, :],
                                         m0[:, QT * b:QT * b + QT].unsqueeze(2).to_broadcast([128, QT, SK]),
                                         ALU.mult))
            dve.wait_ge(pe1, 4)
            for b in range(B):
                stage1(dve.tensor_copy(p0T[:, b, :], TR[b][0:B * SK, :, :].rearrange("p q d -> p (q d)")))
            dve.wait_ge(pe1, 5)
            for b in range(B):
                stage1(dve.tensor_copy(a0T[:, b, :], SC[b][:, :]))
            stage1(dve.tensor_tensor(t[:, :, :], t[:, :, :], rows0_sb[:, 1:2, :].to_broadcast([128, NT, D]),
                                     ALU.add))
            dve.wait_ge(dve1, 18)
            dve.wait_ge(pe1, 6)
            for b in range(B):
                dve.tensor_tensor(t[:, QT * b:QT * b + QT, :], ACC[b][:, :, :], t[:, QT * b:QT * b + QT, :],
                                  ALU.add).then_inc(res_ready, 1)

            def norm_tiles(i, res):
                dve.wait_ge(res_ready, res)
                for j in range(NT):
                    dve.bn_stats(stats[:, j, :], t[:, j, :]).then_inc(ln_stats, 1)
                dve.wait_ge(ln_stats, i * NT + NT)
                dve.sem_inc(dve_passed, 1)
                for j in range(NT):
                    dve.bn_aggr(mv[:, j, :], stats[:, j, :]).then_inc(ln_mv, 1)
                dve.wait_ge(ln_rstd, i + 1)
                for j in range(NT):
                    dve.tensor_scalar(xhat[:, j, :], t[:, j, :], mv[:, j, 0:1], rstd[:, j:j + 1],
                                      ALU.subtract, ALU.mult).then_inc(ln_xhat, 1)

            def residual(i, k):
                for b in range(B):
                    dve.wait_ge(acc_ready, (i - k) * 2 + b + 1)
                    dve.wait_ge(bias_added, (i - k) * 2 + b + 1)
                    dve.tensor_tensor(t[:, QT * b:QT * b + QT, :], ACC[b][:, :, :], t[:, QT * b:QT * b + QT, :],
                                      ALU.add).then_inc(res_ready, 1)

            def low(dst, full, hi, split):
                dve.wait_ge(split_hi, split)
                dve.tensor_tensor(dst, full, hi.bitcast(F32), ALU.subtract).then_inc(fill_read, 1)

            def pair(it, f, spl, last):
                lows = {2: 0, 3: 1}
                for s in range(2 * QT):
                    b, q = divmod(s, QT)
                    n = it * 8 + s
                    for h in range(2):
                        dve.wait_ge(scored[h], n + 1)
                        if s >= 2:
                            dve.wait_ge(expd[h], n - 1)
                        dve.sem_inc(dve_passed, 1)
                        dve.tensor_tensor_reduce(Ms[:, s % 2, h, :], SC[h][:, :], cap[:, s, :], -SCALE, 3.0e38,
                                                 ALU.add, ALU.min, nmax[:, s % 2, h:h + 1]).then_inc(capped[h], 1)
                    if s in lows:
                        h = lows[s]
                        low(Hl[:, 1, h, :], X[:, :], Hh[:, 1, h, :], spl + h + 1)
                    if s == QT:
                        invert(it, 0)
                    if s >= 1:
                        turn_copy(n - 1, s - 1)
                    if s == QT + 1:
                        normalise(it, f + 4, 0)
                s = 2 * QT - 1
                if not last:
                    low(Al[:, :, :].rearrange("p a d -> p (a d)"), X[:, 0:2 * D],
                        Ah[:, :, :].rearrange("p a d -> p (a d)"), spl + 3)
                invert(it, 1)
                turn_copy(it * 8 + s, s)
                if not last:
                    for h in range(2):
                        low(Hl[:, 0, h, :], X[:, :], Hh[:, 0, h, :], spl + 4 + h)
                normalise(it, f + (5 if last else 8), 1)

            def turn_copy(n, s):
                dve.wait_ge(turned[1], n + 1)
                if s >= 2:
                    dve.wait_ge(pv_done, n - 1)
                dve.tensor_copy(PT[:, s % 2, 1, :, :], TR[1][:, :, :]).then_inc(pt_ready[1], 1)

            def invert(it, b):
                for h in range(2):
                    dve.wait_ge(expd[h], it * 8 + QT * b + QT)
                dve.reciprocal(rinv[:, b, :, :], rsum[:, b, :, :]).then_inc(rinv_ready, 1)

            def normalise(it, f, b):
                dve.wait_ge(pv_done, it * 8 + QT * b + QT)
                dve.wait_ge(fill_read, FREE + f + 1)
                dve.tensor_tensor(OT[:, :], O[:, :], Rsb[:, :], ALU.mult).then_inc(ot_ready, 1)

            for k in range(2):
                if k:
                    base = n1
                    dve.wait_ge(pe1, 7)
                    read_T(xT)
                    dve.wait_ge(pe1, 8)
                    queries_keys_values(cols2_sb, rows2_sb, lambda: [stage1(dve.tensor_tensor(
                        v2[SK * b:SK * b + SK, b, :], O[SK * b:SK * b + SK, 0:D],
                        rows2_sb[SK * b:SK * b + SK, 0, :], ALU.add)) for b in range(B)])
                    dve.wait_ge(pe1, 9)
                    stage1(dve.tensor_reduce(m2[:, :], X[0:B * SK, :], AX.X, ALU.max))
                    dve.wait_ge(dve1, base + 8)
                    stage1(dve.tensor_scalar(m2[:, :], m2[:, :], -SCALE1, None, ALU.mult))
                    dve.wait_ge(act1, 2)
                    stage1(dve.reciprocal(m2[:, :], z2[:, :]))
                    dve.wait_ge(dve1, base + 10)
                    stage1(dve.tensor_scalar(p2[:, :], p2[:, :], m2[:, 0:1], None, ALU.mult))
                    dve.wait_ge(pe1, 10)
                    for b in range(B):
                        stage1(dve.tensor_tensor(t[:, QT * b:QT * b + QT, :], ACC[b][:, :, :],
                                                 t[:, QT * b:QT * b + QT, :], ALU.add))
                    dve.wait_ge(dve1, base + 13)
                    norm_tiles(3 * NL, 2 + 6 * NL)
                    dve.wait_ge(ln_xhat, (3 * NL + 1) * NT)
                    stage1(dve.tensor_tensor(xhat[:, :, :], xhat[:, :, :],
                                             rows2_sb[:, 1:2, :].to_broadcast([128, NT, D]), ALU.mult))
                    dve.wait_ge(dve1, base + 14)
                    for b in range(B):
                        dve.tensor_tensor(t[:, QT * b:QT * b + QT, :], xhat[:, QT * b:QT * b + QT, :],
                                          rows2_sb[:, 2:3, :].to_broadcast([128, QT, D]),
                                          ALU.add).then_inc(res_ready, 1)
                with dve.Fori(0, NL) as l:
                    g = l + k * NL
                    i = g * 3 + k
                    norm_tiles(i, (g * 3 + k) * 2 + 2)
                    tn = g * TND
                    dve.wait_ge(ln_xhatT, g * 6 + 1)
                    dve.tensor_scalar(tnT[:, 0, :], TR[0][:, :, :].rearrange("p q d -> p (q d)"),
                                      norm_sb[:, k, 0:1], norm_sb[:, k, 1:2], ALU.mult, ALU.add).then_inc(tn_dve, 1)
                    dve.wait_ge(tn_dve, tn + 1)
                    dve.tensor_copy(tnh[:, 0, :], tnT[:, 0, :]).then_inc(tn_dve, 1)
                    dve.wait_ge(tn_dve, tn + 2)
                    dve.tensor_tensor(tnl[:, 0, :], tnT[:, 0, :], tnh[:, 0, :].bitcast(F32),
                                      ALU.subtract).then_inc(tn_dve, 1)
                    dve.wait_ge(tn_act, g * TNA + 2)
                    dve.tensor_tensor(tnl[:, 1, :], tnT[:, 1, :], tnh[:, 1, :].bitcast(F32),
                                      ALU.subtract).then_inc(tn_dve, 1)
                    sp0 = g * SPLITS
                    low(Al[:, :, :].rearrange("p a d -> p (a d)"), X[:, 0:2 * D],
                        Ah[:, :, :].rearrange("p a d -> p (a d)"), sp0 + 1)
                    for h in range(2):
                        low(Hl[:, 0, h, :], X[:, :], Hh[:, 0, h, :], sp0 + 2 + h)
                    with dve.Fori(0, NP - 1) as p:
                        pair(g * NP + p, g * FILLS + p * 9 + 3, g * SPLITS + p * 5 + 3, False)
                    pair(g * NP + (NP - 1), g * FILLS + (NP - 1) * 9 + 3, g * SPLITS + (NP - 1) * 5 + 3, True)
                    residual(i, k)
                    norm_tiles(i + 1, (g * 3 + k) * 2 + 4)
                    dve.wait_ge(ln_xhatT, g * 6 + 3)
                    dve.tensor_scalar(tnT[:, 0, :], TR[0][:, :, :].rearrange("p q d -> p (q d)"),
                                      norm_sb[:, k, 0:1], norm_sb[:, k, 1:2], ALU.mult, ALU.add).then_inc(tn_dve, 1)
                    for j in range(NT + 1):
                        if j < NT:
                            n = g * NT + j
                            dve.wait_ge(x_scored, n + 1)
                            if j >= 4:
                                dve.wait_ge(x_turned, n - 3)
                            dve.tensor_tensor(XB[:, j % 4, :, :], SC[j % 2][:, :].rearrange("p (h m) -> p h m", h=H),
                                              ccap[:, j // QT:j // QT + 1, :].to_broadcast([128, H, SK]),
                                              ALU.add).then_inc(x_capped, 1)
                            if j >= 2:
                                dve.wait_ge(x_sub, n - 1)
                            dve.wait_ge(x_capped, n + 1)
                            dve.tensor_reduce(xmax[:, j % 2, :], XB[:, j % 4, :, :], AX.X, ALU.max).then_inc(x_max, 1)
                        if j >= 1:
                            n = g * NT + j - 1
                            dve.wait_ge(x_exp, n + 1)
                            dve.tensor_reduce(xsum[:, (j - 1) % 2, :], XB[:, (j - 1) % 4, :, :], AX.X,
                                              ALU.add).then_inc(x_sum, 1)
                            if j >= 3:
                                dve.wait_ge(x_norm, n - 1)
                            dve.wait_ge(x_sum, n + 1)
                            dve.reciprocal(xinv[:, (j - 1) % 2, :], xsum[:, (j - 1) % 2, :]).then_inc(x_inv, 1)
                    residual(i + 1, k)
                    norm_tiles(i + 2, (g * 3 + k) * 2 + 6)
                    dve.wait_ge(ld_ff, (g + 1) * 48)
                    dve.wait_ge(ln_xhatT, g * 6 + 5)
                    dve.tensor_scalar(tnT[:, 0, :], TR[0][:, :, :].rearrange("p q d -> p (q d)"),
                                      cols_sb[:, 0:1], cols_sb[:, 1:2], ALU.mult, ALU.add).then_inc(tn_dve, 1)
                    for m in range(B * NF):
                        if m % 2:
                            dve.wait_ge(ff_h, g * 8 + m + 1)
                            dve.tensor_scalar(hT[:, m % NF, m // NF, :], SC[1][:, :],
                                              cols_sb[:, 2 + m % NF:3 + m % NF], 0.0,
                                              ALU.add, ALU.max).then_inc(ff_relu[1], 1)
                    residual(i + 2, k)

        @block.scalar
        def _(act):
            act.wait_ge(dve1, 9)
            act.activation(s0[:, :, :], s0[:, :, :], ACT.Exp, scale=SCALE1).then_inc(act1, 1)

            def high(dst, src, f):
                act.wait_ge(fill, FREE + f + 1)
                act.activation(dst, src, ACT.Copy).then_inc(split_hi, 1)

            def values(f, b):
                act.wait_ge(fill, FREE + f + 1)
                act.activation(V[:, QT * b:QT * b + QT, :], X[:, :].rearrange("p (j d) -> p j d", j=QT),
                               ACT.Copy).then_inc(fill_read, 1)

            def turn_copy(n, s):
                act.wait_ge(turned[0], n + 1)
                if s >= 2:
                    act.wait_ge(pv_done, n - 1)
                act.activation(PT[:, s % 2, 0, :, :], TR[0][:, :, :], ACT.Copy).then_inc(pt_ready[0], 1)

            def spread_to(f):
                act.wait_ge(fill, FREE + f + 1)
                act.activation(Rsb[:, :], X[:, :], ACT.Copy).then_inc(fill_read, 1)

            def pair(it, f, last):
                for s in range(2 * QT):
                    b, q = divmod(s, QT)
                    n = it * 8 + s
                    for h in range(2):
                        act.wait_ge(capped[h], FREE + n + 1)
                        if s >= 2:
                            act.wait_ge(turned[h], n - 1)
                        act.activation(E[:, s % 2, h, :], Ms[:, s % 2, h, :], ACT.Exp, scale=-1.0,
                                       bias=nmax[:, s % 2, h:h + 1],
                                       accum_out=rsum[:, b, h, q:q + 1]).then_inc(expd[h], 1)
                    if s < 2:
                        values(f + s, s)
                    elif s < 4:
                        high(Hh[:, 1, s - 2, :], X[:, :], f + s)
                    if s >= 1:
                        turn_copy(n - 1, s - 1)
                    if s == QT + 1:
                        spread_to(f + 4)
                s = 2 * QT - 1
                if not last:
                    high(Ah[:, :, :].rearrange("p a d -> p (a d)"), X[:, 0:2 * D], f + 5)
                turn_copy(it * 8 + s, s)
                if not last:
                    for h in range(2):
                        high(Hh[:, 0, h, :], X[:, :], f + 6 + h)
                spread_to(f + (5 if last else 8))

            for k in range(2):
                if k:
                    act.wait_ge(dve1, 18 + 9)
                    act.activation(p2[:, :], X[0:B * SK, :], ACT.Exp, scale=SCALE1, bias=m2[:, 0:1],
                                   accum_out=z2[:, 0:1]).then_inc(act1, 1)
                with act.Fori(0, NL) as l:
                    g = l + k * NL
                    act.wait_ge(ln_xhatT, g * 6 + 2)
                    act.activation(tnT[:, 1, :], TR[1][:, :, :].rearrange("p q d -> p (q d)"), ACT.Identity,
                                   scale=norm_sb[:, k, 0:1], bias=norm_sb[:, k, 1:2]).then_inc(tn_act, 1)
                    act.wait_ge(tn_act, g * TNA + 1)
                    act.activation(tnh[:, 1, :], tnT[:, 1, :], ACT.Copy).then_inc(tn_act, 1)
                    f0 = g * FILLS
                    high(Ah[:, :, :].rearrange("p a d -> p (a d)"), X[:, 0:2 * D], f0)
                    for h in range(2):
                        high(Hh[:, 0, h, :], X[:, :], f0 + 1 + h)
                    with act.Fori(0, NP - 1) as p:
                        pair(g * NP + p, g * FILLS + p * 9 + 3, False)
                    pair(g * NP + (NP - 1), g * FILLS + (NP - 1) * 9 + 3, True)
                    for a, (bank, bd) in enumerate(((X, KBD), (O, VBD))):
                        act.wait_ge(c_kv, g * 2 + a + 1)
                        for h in range(2):
                            act.activation(bd[HD * h:HD * h + HD, :, :, h, :],
                                           bank[HD * h:HD * h + HD, :].rearrange("p (n b m) -> p n b m", n=NP, b=B),
                                           ACT.Copy).then_inc(c_bd, 1)
                    act.wait_ge(c_mn, FREE + g * 2 + 1)
                    for a in range(2):
                        act.activation(Mw[:, :, a * 256:a * 256 + 256].rearrange("p b (n m) -> p n b m", n=4),
                                       SC[a][:, :].rearrange("p (n b m) -> p n b m", n=4, b=B),
                                       ACT.Copy).then_inc(c_mn_sb, 1)
                    act.wait_ge(c_mn, FREE + g * 2 + 2)
                    for b, bank in enumerate((X, O)):
                        act.activation(Nw[:, b, :, :], bank[:, :].rearrange("p (c d) -> p c d", c=4),
                                       ACT.Copy).then_inc(c_mn_sb, 1)
                    act.wait_ge(ln_xhatT, g * 6 + 4)
                    act.activation(tnT[:, 1, :], TR[1][:, :, :].rearrange("p q d -> p (q d)"), ACT.Identity,
                                   scale=norm_sb[:, k, 0:1], bias=norm_sb[:, k, 1:2]).then_inc(tn_act, 1)
                    for j in range(NT + 2):
                        if j < NT:
                            act.wait_ge(x_sub, g * NT + j + 1)
                            act.activation(XB[:, j % 4, :, :], XB[:, j % 4, :, :], ACT.Exp,
                                           scale=SCALE).then_inc(x_exp, 1)
                        if j >= 2:
                            n = g * NT + j - 2
                            act.wait_ge(x_turned, n + 1)
                            if j >= 4:
                                act.wait_ge(x_out, n - 1)
                            act.activation(PX[:, j % 2, :, :], TR[j % 2][:, :, :], ACT.Copy).then_inc(x_pt, 1)
                    act.wait_ge(ld_ff, (g + 1) * 48)
                    act.wait_ge(ln_xhatT, g * 6 + 6)
                    act.activation(tnT[:, 1, :], TR[1][:, :, :].rearrange("p q d -> p (q d)"), ACT.Identity,
                                   scale=cols_sb[:, 0:1], bias=cols_sb[:, 1:2]).then_inc(tn_act, 1)
                    for m in range(0, B * NF, 2):
                        act.wait_ge(ff_h, g * 8 + m + 1)
                        act.activation(hT[:, m % NF, m // NF, :], SC[0][:, :], ACT.Relu,
                                       bias=cols_sb[:, 2 + m % NF:3 + m % NF]).then_inc(ff_relu[0], 1)

        @block.tensor
        def _(pe):
            def three(out_, wh, wl, mh, ml, inc=None):
                pe.matmul(out_, wh, ml, start=True, stop=False)
                pe.matmul(out_, wl, mh, start=False, stop=False)
                return pe.matmul(out_, wh, mh, start=False, stop=True)

            def turn_tokens(src):
                for b in range(B):
                    for q in range(QT):
                        ins = pe.transpose(TR[b][:, q, :], src[:, QT * b + q, :], ident[:, :])
                return ins

            def queries_keys_values(w, wkv):
                for b in range(B):
                    pe.matmul(SC[b][:, :], w[:, 0, :], xT[:, b, :], start=True, stop=True)
                pe.matmul(X[:, 0:B * SK], wkv[:, 0, :], ctxT[:, :], start=True, stop=True)
                return pe.matmul(O[0:B * SK, 0:D], ctxT[:, :], wkv[:, 1, :], start=True, stop=True)

            for free in (*capped, *pt_ready, fill_read):
                pe.sem_inc(free, FREE)

            pe.wait_ge(const_ready, 4)
            pe.wait_ge(ld_in, 64)
            pe.transpose(X[0:DK, 0:B * SK], ctx_sb[:, :], ident[0:B * SK, 0:B * SK])
            turn_tokens(t).then_inc(pe1, 1)
            pe.wait_ge(dve1, 3)
            pe.wait_ge(ld_w0, 144)
            queries_keys_values(w0_sb, w0kv_sb).then_inc(pe1, 1)
            pe.wait_ge(dve1, 7)
            for j in range(NT):
                b, q = divmod(j, QT)
                mm = pe.matmul(X[:, j * SK:j * SK + SK], q0T[:, b, q * 128:q * 128 + 128],
                               k0T[:, b * SK:b * SK + SK], start=True, stop=True)
            mm.then_inc(pe1, 1)
            pe.wait_ge(dve1, 13)
            for j in range(NT):
                b, q = divmod(j, QT)
                mm = pe.transpose(TR[b][0:B * SK, q, :], p0[:, j, :], ident[:, :])
            mm.then_inc(pe1, 1)
            pe.wait_ge(dve1, 15)
            for b in range(B):
                mm = pe.matmul(SC[b][:, :], v0[:, :], p0T[:, b, :], start=True, stop=True)
            mm.then_inc(pe1, 1)
            pe.wait_ge(dve1, 17)
            for j in range(NT):
                b, q = divmod(j, QT)
                mm = pe.matmul(ACC[b][:, q, :], a0T[:, b, q * 128:q * 128 + 128], w0_sb[:, 1, :],
                               start=True, stop=True)
            mm.then_inc(pe1, 1)

            def turn_normed(i):
                for b in range(B):
                    pe.wait_ge(ln_xhat, i * NT + QT * b + QT)
                    for q in range(QT):
                        ins = pe.transpose(TR[b][:, q, :], xhat[:, QT * b + q, :], ident[:, :])
                    ins.then_inc(ln_xhatT, 1)

            def fold_qk(it, f):
                pe.wait_ge(ld_wqk, (it + 1) * 16)
                pe.wait_ge(fill_read, FREE + f)
                for h in range(2):
                    mm = pe.matmul(X[:, h * D:h * D + D], wqk_sb[:, 1, h, :], wqk_sb[:, 0, h, :], start=True, stop=True)
                    if h == 1:
                        mm.then_inc(fill, 1)

            def keys(f, b, h):
                pe.wait_ge(fill_read, FREE + f)
                three(X[:, :], Ah[:, h, :], Al[:, h, :], tnh[:, b, :], tnl[:, b, :]).then_inc(fill, 1)

            def values(it, f, b):
                if b == 0:
                    pe.wait_ge(ld_wv, (it + 1) * 16)
                pe.wait_ge(fill_read, FREE + f)
                for q in range(QT):
                    mm = pe.matmul(X[:, q * 128:q * 128 + 128], tnT[:, b, q * 128:q * 128 + 128], wv_sb[:, :],
                                   start=True, stop=True)
                mm.then_inc(fill, 1)

            def scores(n, s):
                b, q = divmod(s, QT)
                for h in range(2):
                    pe.wait_ge(capped[h], FREE + n)
                    three(SC[h][:, :], tnh[:, b, q * 128:q * 128 + 128], tnl[:, b, q * 128:q * 128 + 128],
                          Hh[:, b, h, :], Hl[:, b, h, :]).then_inc(scored[h], 1)

            def turn(n, s):
                for h in range(2):
                    pe.wait_ge(expd[h], n + 1)
                    pe.wait_ge(pt_ready[h], FREE + n)
                    for c in range(KT):
                        mm = pe.transpose(TR[h][:, c, :], E[:, s % 2, h, c * 128:c * 128 + 128], ident[:, :])
                    mm.then_inc(turned[h], 1)

            def times_v(n, s):
                b, q = divmod(s, QT)
                for h in range(2):
                    pe.wait_ge(pt_ready[h], FREE + n + 1)
                for c in range(KT):
                    for h in range(2):
                        mm = pe.matmul(O[HD * h:HD * h + HD, q * 128:q * 128 + 128],
                                       V[:, QT * b + c, HD * h:HD * h + HD], PT[:, s % 2, h, c, :],
                                       start=(c == 0), stop=(c == KT - 1))
                mm.then_inc(pv_done, 1)

            def spread(it, f, b):
                pe.wait_ge(rx_ready, it * 2 + b + 1)
                pe.wait_ge(fill_read, FREE + f)
                for q in range(QT):
                    mm = pe.transpose(X[:, q * 128:q * 128 + 128],
                                      rx[:, q, :, :].rearrange("p h d -> p (h d)"), ident[:, :])
                mm.then_inc(fill, 1)

            def project(it, b):
                pe.wait_ge(ot_ready, it * 2 + b + 1)
                if b == 0:
                    pe.wait_ge(ld_wo, (it + 1) * 16)
                for q in range(QT):
                    mm = pe.matmul(ACC[b][:, q, :], OT[:, q * 128:q * 128 + 128], wo_sb[:, :],
                                   start=False, stop=False, skip_group_check=True)
                return mm

            def pair(it, f, last):
                for s in range(2 * QT):
                    n = it * 8 + s
                    if s == 0:
                        pe.wait_ge(fill_read, FREE + f)
                    if s == QT:
                        pe.wait_ge(fill_read, FREE + f + 4)
                    scores(n, s)
                    if s < 2:
                        values(it, f + s, s)
                    elif s < 4:
                        keys(f + s, 1, s - 2)
                    if s >= 1:
                        turn(n - 1, s - 1)
                    if s >= 2:
                        if s == QT + 2:
                            pe.wait_ge(ot_ready, it * 2 + 1)
                        times_v(n - 2, s - 2)
                    if s == QT + 1:
                        spread(it, f + 4, 0)
                    if s == QT + 2:
                        project(it, 0)
                n = it * 8 + 2 * QT - 1
                if not last:
                    fold_qk(it + 1, f + 5)
                turn(n, 2 * QT - 1)
                times_v(n - 1, 2 * QT - 2)
                if not last:
                    for h in range(2):
                        keys(f + 6 + h, 0, h)
                times_v(n, 2 * QT - 1)
                spread(it, f + (5 if last else 8), 1)
                return project(it, 1)

            for k in range(2):
                if k:
                    d1 = 18
                    pe.wait_ge(res_ready, 2 + 6 * NL)
                    turn_tokens(t).then_inc(pe1, 1)
                    pe.wait_ge(dve1, d1 + 2)
                    queries_keys_values(w2_sb, w2kv_sb).then_inc(pe1, 1)
                    pe.wait_ge(dve1, d1 + 7)
                    for b in range(B):
                        mm = pe.matmul(X[SK * b:SK * b + SK, :], k0T[:, SK * b:SK * b + SK], q0T[:, b, :],
                                       start=True, stop=True)
                    mm.then_inc(pe1, 1)
                    pe.wait_ge(dve1, d1 + 11)
                    for j in range(NT):
                        b, q = divmod(j, QT)
                        mm = pe.matmul(ACC[b][:, q, :], p2[:, q * 128:q * 128 + 128], v2[:, b, :],
                                       start=True, stop=True)
                    mm.then_inc(pe1, 1)
                with pe.Fori(0, NL) as l:
                    g = l + k * NL
                    i = g * 3 + k
                    f0 = g * FILLS
                    fold_qk(g * NP, f0)
                    pe.wait_ge(res_ready, (g * 3 + k) * 2 + 2)
                    for b in range(B):
                        pe.matmul(ACC[b][:, :, :].rearrange("p q d -> p (q d)"), zeros[:, 0:128], zeros[:, :],
                                  start=True, stop=False, skip_group_check=True)
                    turn_normed(i)
                    pe.wait_ge(tn_dve, g * TND + 3)
                    keys(f0 + 1, 0, 0)
                    pe.wait_ge(tn_dve, g * TND + 4)
                    keys(f0 + 2, 0, 1)
                    with pe.Fori(0, NP - 1) as p:
                        it = g * NP + p
                        pair(it, g * FILLS + p * 9 + 3, False).then_inc(wo_used, 1)
                    pair(g * NP + (NP - 1), g * FILLS + (NP - 1) * 9 + 3, True).then_inc(wo_used, 1)
                    for b in range(B):
                        pe.matmul(ACC[b][:, :, :].rearrange("p q d -> p (q d)"), zeros[:, 0:128], zeros[:, :],
                                  start=False, stop=True, skip_group_check=True).then_inc(acc_ready, 1)
                    pe.wait_ge(ld_ckv, (g + 1) * 16)
                    pe.wait_ge(bd_zero, 4)
                    for a, bank in enumerate((X, O)):
                        for n in range(NP):
                            mm = pe.matmul(bank[:, n * 64:n * 64 + 64], ckv_sb[:, a, n, :], ctxT[:, :],
                                           start=True, stop=True)
                        mm.then_inc(c_kv, 1)
                    pe.wait_ge(ld_cqo, (g + 1) * 16)
                    pe.wait_ge(c_bd, g * 4 + 2)
                    for n in range(NP):
                        mm = pe.matmul(SC[n // 4][:, (n % 4) * 128:(n % 4) * 128 + 128], cqo_sb[:, 0, n, :],
                                       KBD[:, n, :, :, :].rearrange("p b h m -> p (b h m)"), start=True, stop=True)
                    mm.then_inc(c_mn, 1)
                    pe.wait_ge(c_bd, g * 4 + 4)
                    for b, bank in enumerate((X, O)):
                        for n in range(NP):
                            mm = pe.matmul(bank[64 * (n % 2):64 * (n % 2) + 64, (n // 2) * D:(n // 2) * D + D],
                                           VBD[:, n, b, :, :].rearrange("p h m -> p (h m)"), cqo_sb[:, 1, n, :],
                                           start=True, stop=True)
                    mm.then_inc(c_mn, 1)
                    turn_normed(i + 1)
                    pe.wait_ge(c_mn_sb, g * 4 + 4)
                    pe.wait_ge(tn_dve, g * TND + 5)
                    pe.wait_ge(tn_act, g * TNA + 3)
                    pe.wait_ge(res_ready, (g * 3 + k) * 2 + 4)
                    for j in range(NT + 3):
                        if j < NT:
                            n = g * NT + j
                            if j >= 2:
                                pe.wait_ge(x_capped, n - 1)
                            pe.matmul(SC[j % 2][:, :], tnT[:, j // QT, (j % QT) * 128:(j % QT) * 128 + 128],
                                      Mw[:, j // QT, :], start=True, stop=True).then_inc(x_scored, 1)
                        if 2 <= j < NT + 2:
                            n = g * NT + j - 2
                            pe.wait_ge(x_norm, n + 1)
                            if j >= 4:
                                pe.wait_ge(x_pt, n - 1)
                            xb = XB[:, (j - 2) % 4, :, :].rearrange("p h m -> p (h m)")
                            for c in range(4):
                                mm = pe.transpose(TR[j % 2][:, c, :], xb[:, c * 128:c * 128 + 128], ident[:, :])
                            mm.then_inc(x_turned, 1)
                        if j >= 3:
                            b, q = divmod(j - 3, QT)
                            n = g * NT + j - 3
                            pe.wait_ge(x_pt, n + 1)
                            for c in range(4):
                                mm = pe.matmul(ACC[b][:, q, :], PX[:, (j - 3) % 2, c, :], Nw[:, b, c, :],
                                               start=(c == 0), stop=(c == 3))
                            mm.then_inc(x_out, 1)
                            if q == QT - 1:
                                pe.matmul(X[:, 0:128], zeros[:, 0:128], zeros[:, 0:128], start=True,
                                          stop=True).then_inc(acc_ready, 1)
                    turn_normed(i + 2)
                    pe.wait_ge(ld_ff, (g + 1) * 48)
                    for m in range(B * NF):
                        b, c = divmod(m, NF)
                        if m == 0:
                            pe.wait_ge(tn_dve, g * TND + 6)
                        if m == NF:
                            pe.wait_ge(tn_act, g * TNA + 4)
                        if m >= 2:
                            pe.wait_ge(ff_relu[m % 2], g * 4 + m // 2)
                        pe.matmul(SC[m % 2][:, :], ffw_sb[:, 0, c * 128:c * 128 + 128], tnT[:, b, :],
                                  start=True, stop=True).then_inc(ff_h, 1)
                    pe.wait_ge(res_ready, (g * 3 + k) * 2 + 6)
                    for b in range(B):
                        for e in range(2):
                            pe.wait_ge(ff_relu[e], g * 4 + 2 * b + 2)
                        for q in range(QT):
                            for c in range(NF):
                                mm = pe.matmul(ACC[b][:, q, :], hT[:, c, b, q * 128:q * 128 + 128],
                                               ffw_sb[:, 1, c * 128:c * 128 + 128], start=(c == 0),
                                               stop=(c == NF - 1))
                        mm.then_inc(acc_ready, 1)


def kernel(**inputs):
    import numpy as np
    import concourse.bacc as bacc
    from concourse.bass_utils import run_bass_kernel_spmd

    a = {k: np.asarray(v) for k, v in inputs.items()}
    stacks = ("L1_xattn_", "L3_xattn_")

    def both(name):
        return np.concatenate([a[s + name] for s in stacks])

    G = 2 * NL
    wqT = both("sa_q").transpose(0, 2, 1).reshape(G * NP, 2, HD, D)
    wkT = both("sa_kv")[:, :, :H * HD].transpose(0, 2, 1).reshape(G * NP, 2, HD, D)
    wv = both("sa_kv")[:, :, H * HD:].reshape(G, D, NP, 128).transpose(0, 2, 1, 3).reshape(G * NP, D, 128)
    wo = both("sa_ow").reshape(G * NP, 128, D)
    cqT = both("ca_q").transpose(0, 2, 1).reshape(G, NP, 128, D)
    co = both("ca_ow").reshape(G, NP, 128, D)
    w2f = both("ff_w2").reshape(G, NF, 128, D).transpose(0, 2, 1, 3).reshape(G, 128, NF * D)
    arrays = {
        "x": a["x"], "ctx": a["ctx_512"], "mask": a["mask_BxSxS_ik0"], "cmask": a["mask_Bx1xS2_if1"],
        "w0": np.stack([a["L0_xattn_Wq"], a["L0_xattn_Wo"]], 1),
        "w0kv": np.stack([a["L0_xattn_Wk"], a["L0_xattn_Wv"]], 1),
        "w2": a["L2_xattn_Wq"][:, None, :],
        "w2kv": np.stack([a["L2_xattn_Wk"], a["L2_xattn_Wv"]], 1),
        "rows0": np.stack([a["L0_xattn_bv"], a["L0_xattn_bo"]]),
        "rows2": np.stack([a["L2_xattn_bv"], a["L2_xattn_gamma"], a["L2_xattn_beta"]]),
        "cols0": np.stack([a["L0_xattn_bq"], a["L0_xattn_bk"]], 1),
        "cols2": np.stack([a["L2_xattn_bq"], a["L2_xattn_bk"]], 1),
        "wqk": np.stack([wqT, wkT], 1).transpose(0, 3, 1, 2, 4), "wv": wv, "wo": wo,
        "ckv": both("ca_kv").reshape(G, DK, 2, NP, 128),
        "cqo": np.stack([cqT, co], 1).transpose(0, 3, 1, 2, 4),
        "ffw": np.stack([both("ff_w1"), w2f], 2),
        "cols": np.concatenate([both("pre_g")[:, :, None], both("pre_b")[:, :, None],
                                both("ff_b1").reshape(G, NF, 128).transpose(0, 2, 1)], 2),
        "rows": np.stack([both("sa_ob"), both("ca_ob"), both("ff_b2")], 1),
        "norms": np.stack([np.stack([a[s + "norm_g"], a[s + "norm_b"]], 1) for s in stacks], 1),
    }
    arrays = {k: np.ascontiguousarray(v) for k, v in arrays.items()}
    nc = bacc.Bacc("TRN2", target_bir_lowering=False, num_devices=1)
    aps = {k: nc.dram_tensor(k, v.shape, mybir.dt.from_np(v.dtype), kind="ExternalInput").ap()
           for k, v in arrays.items()}
    out = nc.dram_tensor("out", (B, S, D), F32, kind="ExternalOutput").ap()
    build(nc, out=out, **aps)
    r = run_bass_kernel_spmd(nc, [arrays], core_ids=[0])
    return r.results[0]["out"]
```

```python
from contextlib import ExitStack

import concourse.bass as bass
from concourse import mybir

F32 = mybir.dt.float32
F32R = mybir.dt.float32r
I32 = mybir.dt.int32
ALU = mybir.AluOpType
ACT = mybir.ActivationFunctionType
AX = mybir.AxisListType

B = 2
S = 512
D = 128
SK = 32
DK = 64
H = 16
HD = 64
NP = H // 2
FF = 512
NL = 6
QT = S // 128
NT = B * QT
KT = S // 128
NF = FF // 128
SCALE = HD ** -0.5
MASKED = -1.0e30
SCALE1 = 128 ** -0.5
EPS = 1e-5
EPS2 = 1e-6

FREE = 1

STEPS = NP * QT

SELF_DONE, NORM1 = 3, 4
CROSS = (7, 7, 8, 10)
CROSS_EXP, CROSS_SUM = 1, 2
CROSS_OUT = (12, 12, 13, 15)
CROSS_DONE, NORM2 = 16, 17
FF_OUT = 23
FF_DONE, NORM0, SPLIT0 = 25, 26, 28

REST = {"T1": (6, 1), "S0": (7, 0), "S1": (7, 1), "S2": (8, 2), "S3": (10, 1),
        "P0": (11, 0), "P1": (11, 1), "P2": (12, 2), "P3": (14, 1),
        "T2": (18, 1), "F0": (19, 0), "F1": (19, 1), "F2": (20, 2), "F3": (22, 1), "T0": (27, 0)}
FOLD = {"K": (23, 0), "U": (23, 1), "M0": (24, 2), "M1": (26, 1), "N0": (27, 1), "N1": (30, 1)}

FIRST = (False, True, False, True)
MIDDLE = (True, True, True, True)
LAST = (True, True, True, False)
DRAIN = (True, False, True, False)


def slots(kind, b):
    carry, own, rest, more = kind
    at = {}

    def put(where, name):
        assert where not in at
        at[where] = name

    for p in range(NP):
        s = p * QT
        if own:
            put((s, 0), f"V{p}")
            if p < NP - 1 if b == 0 else p == NP - 1 and more:
                put((s, 1), f"A{p + 1}")
            if p < NP - 1 or more:
                put((s + 1, 1), f"H{p + 1}0")
                put((s + 2, 0), f"H{p + 1}1")
        if (p > 0 or carry) and (own or p == 0):
            put((s + 1, 0), f"R{p - 1}")
    if rest:
        for name, where in REST.items():
            if name != "T0" or more:
                put(where, name)
        if b == 0 and more:
            for name, where in FOLD.items():
                put(where, name)
    return at


def fills(kind, b):
    at = slots(kind, b)
    return [at[where] for where in sorted(at)]


ENTRY = ["A0", "T00", "H00", "H01", "T01", *FOLD]


class Count:

    def __init__(self, k, layer, b, kind, trip=0):
        self.k, self.layer = k, layer
        self.g = layer + k * NL
        self.b, self.kind = b, kind
        self.slots = slots(kind, b)
        self.order = fills(kind, b)
        first, odd, even = (len(fills(*x)) for x in ((FIRST, 0), (MIDDLE, 1), (MIDDLE, 0)))
        last, drain = len(fills(LAST, 1)), len(fills(DRAIN, 0))
        stack = len(ENTRY) + first + (NL - 1) * (odd + even) + last + drain
        base = k * stack + len(ENTRY)
        if kind == FIRST:
            self.base = base
        elif kind == MIDDLE:
            self.base = base + first + trip * (odd + even) + (odd if b == 0 else 0)
        else:
            self.base = base + first + (NL - 1) * (odd + even) + (last if kind == DRAIN else 0)
        self.entry = k * stack
        self.rb = 1 - b
        self.rg = self.g if b else self.g - 1
        rests = trip * 2 + (1 if b == 0 else 0) if kind == MIDDLE else 2 * (NL - 1) + (kind == DRAIN)
        self.norm = k * (2 + 6 * NL) + 2 + rests * 3 - (kind == DRAIN)
        self.step = (self.g * 2 + b) * STEPS
        self.pair = (self.g * 2 + b) * NP

    def fill(self, name):
        return self.base + self.order.index(name)

    def split(self, name):
        splits = [x for x in self.order if x[0] in "AH"]
        odd, even = (sum(x[0] in "AH" for x in fills(MIDDLE, b)) for b in (1, 0))
        last = sum(x[0] in "AH" for x in fills(LAST, 1))
        stack = 3 + even + (NL - 1) * (odd + even) + last
        return self.k * stack + 3 + self.layer * (odd + even) + self.b * even + splits.index(name)


def build(nc, x, ctx, mask, cmask, w0, w0kv, w2, w2kv, rows0, rows2, cols0, cols2, wqk, wvo, ckv, cqo, ffw, cols, rows,
          norms, out):
    st = ExitStack()
    with st:
        def sb(name, shape, dt=F32):
            return st.enter_context(nc.sbuf_tensor(name, shape, dt))

        def sem(name):
            return st.enter_context(nc.semaphore(name))

        t = sb("t", [128, NT, D])
        cap = sb("cap", [128, NT, S])
        ccap = sb("ccap", [128, B, SK])
        ident = sb("ident", [128, 128])
        neghalf = sb("neghalf", [128, NT])
        ctx_sb = sb("ctx_sb", [B * SK, DK])
        ctxT = sb("ctxT", [DK, B * SK])
        norm_sb = sb("norm_sb", [128, 2, 2])
        rows_sb = sb("rows_sb", [128, 2 * NL * 3, D])
        stats = sb("stats", [128, NT, 6])
        mv = sb("mv", [128, NT, 2])
        vpe = sb("vpe", [128, NT])
        rstd = sb("rstd", [128, NT])
        xhat = sb("xhat", [128, NT, D])
        tnT = sb("tnT", [128, B, S])
        tnh = sb("tnh", [128, B, S], F32R)
        tnl = sb("tnl", [128, B, S], F32R)
        wqk_sb = sb("wqk_sb", [HD, NP, 2, 2, D])
        wvo_sb = sb("wvo_sb", [128, NP, 2, 128])
        Ah = sb("Ah", [128, NP, 2, D], F32R)
        Al = sb("Al", [128, NP, 2, D], F32R)
        Hh = sb("Hh", [128, 2, 2, S], F32R)
        Hl = sb("Hl", [128, 2, 2, S], F32R)
        V = sb("V", [128, 2, KT, 128])
        Ms = sb("Ms", [128, 2, 2, S])
        nmax = sb("nmax", [128, 2, 2])
        E = sb("E", [128, 2, 2, S])
        rsum = sb("rsum", [128, 2, 2, QT])
        rinv = sb("rinv", [128, 2, 2, QT])
        rx = sb("rx", [128, QT, 2, HD])
        PT = sb("PT", [128, 2, 2, KT, 128])
        Rsb = sb("Rsb", [128, S])
        OT = sb("OT", [128, S])
        ckv_sb = sb("ckv_sb", [DK, 2, NP, 128])
        cqo_sb = sb("cqo_sb", [128, 2, NP, D])
        KBD = sb("KBD", [128, NP, B, 2, SK])
        VBD = sb("VBD", [128, NP, B, 2, SK])
        Mw = sb("Mw", [128, B, H * SK])
        Nw = sb("Nw", [128, B, 4, D])
        XB = sb("XB", [128, QT, H, SK])
        xmax = sb("xmax", [128, QT, H])
        xsum = sb("xsum", [128, QT, H])
        xinv = sb("xinv", [128, QT, H])
        PX = sb("PX", [128, 2, 4, 128])
        ffw_sb = sb("ffw_sb", [128, 2, FF])
        cols_sb = sb("cols_sb", [128, 2 + NF])
        hT = sb("hT", [128, NF, S])
        cm_sb = sb("cm_sb", [128, B, SK], I32)
        w0_sb = V[:, 0, 0:2, :]
        w0kv_sb = V[0:DK, 0, 2:4, :]
        w2_sb = sb("w2_sb", [128, 1, 128])
        w2kv_sb = sb("w2kv_sb", [DK, 2, 128])
        rows0_sb = V[:, 1, 0:2, :]
        rows2_sb = sb("rows2_sb", [128, 3, D])
        cols0_sb = sb("cols0_sb", [128, 2])
        cols2_sb = sb("cols2_sb", [128, 2])
        xT = E[:, 0, :, :]
        q0T = E[:, 1, :, :]
        k0T = sb("k0T", [128, B * SK])
        v0 = sb("v0", [B * SK, D])
        v2 = sb("v2", [B * SK, B, D])
        s0 = XB[:, 0, :, :].rearrange("p (j i) m -> p j (i m)", j=NT)[:, :, 0:SK]
        p0 = hT[:, 0, :].rearrange("p (j m) -> p j m", j=NT)
        m0 = sb("m0", [128, NT])
        z0 = sb("z0", [128, NT])
        p0T = Ms[0:B * SK, 0, :, :]
        a0T = Ms[:, 1, :, :]
        p2 = hT[0:B * SK, 1, :]
        m2 = sb("m2", [B * SK, 1])
        z2 = sb("z2", [B * SK, 1])

        SC = [st.enter_context(nc.psum_tensor(f"SC{h}", [128, S], F32)) for h in range(2)]
        TR = [st.enter_context(nc.psum_tensor(f"TR{h}", [128, 4, 128], F32)) for h in range(2)]
        O = st.enter_context(nc.psum_tensor("O", [128, S], F32))
        X = st.enter_context(nc.psum_tensor("X", [128, S], F32))
        ACC = [st.enter_context(nc.psum_tensor(f"ACC{b}", [128, QT, D], F32)) for b in range(B)]

        ld_in = sem("ld_in")
        ld_mask = sem("ld_mask")
        ld_w0 = sem("ld_w0")
        ld_w2 = sem("ld_w2")
        const_ready = sem("const_ready")
        cap_ready = sem("cap_ready")
        bd_zero = sem("bd_zero")
        pe1 = sem("pe1_products")
        dve1 = sem("dve1_stages")
        act1 = sem("act1_stages")
        res_ready = [sem(f"res_ready{b}") for b in range(B)]
        bias_added = [sem(f"bias_added{b}") for b in range(B)]
        ln_stats = sem("ln_stats")
        ln_mv = sem("ln_mv")
        ln_vpe = sem("ln_vpe")
        ln_rstd = sem("ln_rstd")
        ln_xhat = sem("ln_xhat")
        tn_high = [sem(f"tn_high{b}") for b in range(B)]
        tn_low = [sem(f"tn_low{b}") for b in range(B)]
        ld_wqk = sem("ld_wqk")
        ld_wvo = sem("ld_wvo")
        ld_c = sem("ld_c")
        ld_ff = sem("ld_ff")
        ld_rows = sem("ld_rows")
        fill = sem("spare_filled")
        fill_read = sem("spare_read")
        split_hi = sem("split_hi")
        scored = [sem(f"scored{h}") for h in range(2)]
        capped = [sem(f"capped{h}") for h in range(2)]
        expd = [sem(f"expd{h}") for h in range(2)]
        turned = [sem(f"turned{h}") for h in range(2)]
        pt_ready = [sem(f"pt_ready{h}") for h in range(2)]
        pv_done = sem("pv_done")
        rinv_ready = sem("rinv_ready")
        rx_ready = sem("rx_ready")
        ot_ready = sem("ot_ready")
        projected = sem("projected")
        x_max = sem("x_max")
        x_sub = sem("x_sub")
        x_exp = sem("x_exp")
        x_sum = sem("x_sum")
        x_inv = sem("x_inv")
        x_norm = sem("x_norm")
        x_out = sem("x_out")
        ff_out = sem("ff_out")
        dve_passed = sem("dve_passed")
        pool_passed = sem("pool_passed")
        stored = sem("stored")

        block = st.enter_context(nc.Block())

        def each_half(eng, k, half):
            half(Count(k, 0, 0, FIRST))
            with eng.Fori(0, NL - 1) as l:
                half(Count(k, l, 1, MIDDLE, l))
                half(Count(k, l + 1, 0, MIDDLE, l))
            half(Count(k, NL - 1, 1, LAST))
            half(Count(k, NL, 0, DRAIN))

        def flat(ap):
            return ap.rearrange("p a d -> p (a d)")

        def tiles(a, b):
            return a[:, QT * b:QT * b + QT, :]

        def before(c, p):
            carry, own, _, _ = c.kind
            return (p > 0 or carry) and (own or p == 0)

        @block.sync
        def _(sp):
            sp.sem_inc(ff_out, FREE)

            def attention_weights(g):
                sp.dma_start(wqk_sb[:, :, :, :, :], wqk[bass.ds(g, 1), :, :, :, :, :]
                             .rearrange("o p n a h d -> (o p) n a h d")).then_inc(ld_wqk, 16)

            def pair_weights(it, p, first=False):
                if not first:
                    sp.wait_ge(ld_wvo, it * 16)
                sp.dma_start(wvo_sb[:, p, :, :], wvo[bass.ds(it, 1), :, :, :]
                             .rearrange("o p a d -> (o p) a d")).then_inc(ld_wvo, 16)

            def cross_weights(g):
                sp.dma_start(ckv_sb[:, :, :, :], ckv[bass.ds(g, 1), :, :, :, :]
                             .rearrange("o p a n d -> (o p) a n d")).then_inc(ld_c, 16)
                sp.dma_start(cqo_sb[:, :, :, :], cqo[bass.ds(g, 1), :, :, :, :]
                             .rearrange("o p a n d -> (o p) a n d")).then_inc(ld_c, 16)

            def ff_weights(g):
                sp.wait_ge(ff_out, FREE + g * 2)
                sp.dma_start(ffw_sb[:, :, :], ffw[bass.ds(g, 1), :, :, :]
                             .rearrange("o p a n -> (o p) a n")).then_inc(ld_ff, 16)
                sp.dma_start(cols_sb[:, :], cols[bass.ds(g, 1), :, :]
                             .rearrange("o p n -> (o p) n")).then_inc(ld_ff, 16)

            sp.dma_start(t[:, :, :], x.rearrange("b (q p) d -> p (b q) d", p=128)).then_inc(ld_in, 16)
            sp.dma_start(ctx_sb[:, :], ctx.rearrange("b m d -> (b m) d")).then_inc(ld_in, 16)
            sp.dma_start(w0_sb[:, :, :], w0).then_inc(ld_w0, 16)
            sp.dma_start(w0kv_sb[:, :, :], w0kv).then_inc(ld_w0, 16)
            sp.dma_start(cols0_sb[:, :], cols0).then_inc(ld_w0, 16)
            sp.dma_start(rows0_sb[:, :, :], rows0.partition_broadcast(128)).then_inc(ld_w0, 16)
            sp.dma_start(w2_sb[:, :, :], w2).then_inc(ld_w2, 16)
            sp.dma_start(w2kv_sb[:, :, :], w2kv).then_inc(ld_w2, 16)
            sp.dma_start(cols2_sb[:, :], cols2).then_inc(ld_w2, 16)
            sp.dma_start(rows2_sb[:, :, :], rows2.partition_broadcast(128)).then_inc(ld_w2, 16)
            sp.dma_start(norm_sb[:, :, :], norms).then_inc(ld_w2, 16)
            sp.dma_start(cm_sb[:, :, :],
                         cmask.rearrange("b o m -> (b o) m").partition_broadcast(128)).then_inc(ld_mask, 16)
            sp.dma_start(cap[:, :, :].bitcast(I32), mask.rearrange("b (q p) k -> p (b q) k", p=128)).then_inc(ld_mask, 16)
            for k in range(2):
                g0 = k * NL
                if k:
                    sp.wait_ge(projected, g0 * 2 * NP)
                attention_weights(g0)
                for p in range(NP):
                    pair_weights(g0 * NP + p, p, k == 0 and p == 0)
                cross_weights(g0)
                if k == 0:
                    sp.dma_start(rows_sb[:, :, :], rows.rearrange("g a n -> (g a) n")
                                 .partition_broadcast(128)).then_inc(ld_rows, 16)
                with sp.Fori(0, NL - 1) as l:
                    g = l + g0
                    ff_weights(g)
                    sp.wait_ge(scored[0], (g * 2 + 1) * STEPS)
                    attention_weights(g + 1)
                    cross_weights(g + 1)
                    for p in range(NP):
                        sp.wait_ge(projected, (g * 2 + 1) * NP + p + 1)
                        pair_weights((g + 1) * NP + p, p)
                ff_weights(g0 + NL - 1)
            for b in range(B):
                sp.wait_ge(res_ready[b], 2 + 6 * NL)
                sp.dma_start(out[b:b + 1, :, :].rearrange("b (q p) d -> p (b q) d", p=128),
                             tiles(t, b)).then_inc(stored, 16)
            sp.wait_ge(stored, 32)

        @block.gpsimd
        def _(pool):
            pool.memset(ident[:, :], 0.0).then_inc(const_ready, 1)
            pool.wait_ge(const_ready, 1)
            pool.affine_select(out=ident[:, :], in_=ident[:, :], compare_op=ALU.not_equal, fill=1.0,
                               base=0, pattern=[[-1, 128]], channel_multiplier=1).then_inc(const_ready, 1)
            pool.memset(neghalf[:, :], -0.5).then_inc(const_ready, 1)
            pool.memset(p0[:, :, :], 0.0).then_inc(bd_zero, 1)
            pool.memset(v2[:, :, :], 0.0).then_inc(bd_zero, 1)
            pool.memset(KBD[:, :, :, :, :], 0.0).then_inc(bd_zero, 1)
            pool.memset(VBD[:, :, :, :, :], 0.0).then_inc(bd_zero, 1)

            def norm_factor(e, b, eps):
                pool.wait_ge(ln_mv, e + 1)
                pool.sem_inc(pool_passed, 1)
                pool.tensor_scalar(vpe[:, QT * b:QT * b + QT], tiles(mv, b)[:, :, 1:2].rearrange("p j o -> p (j o)"),
                                   eps, None, ALU.add).then_inc(ln_vpe, 1)
                pool.wait_ge(ln_vpe, e + 1)
                pool.tensor_tensor(rstd[:, QT * b:QT * b + QT], vpe[:, QT * b:QT * b + QT],
                                   neghalf[:, QT * b:QT * b + QT], ALU.pow).then_inc(ln_rstd, 1)

            def add_bias(e, b, row):
                pool.wait_ge(ln_xhat, e + 1)
                pool.sem_inc(pool_passed, 1)
                pool.tensor_tensor(tiles(t, b), tiles(t, b),
                                   rows_sb[:, bass.ds(row, 1), :].to_broadcast([128, QT, D]),
                                   ALU.add).then_inc(bias_added[b], 1)

            def half(c):
                carry, own, rest, more = c.kind
                rb, rg = c.rb, c.rg
                for s in range(STEPS):
                    p, q = divmod(s, QT)
                    if q == 0 and before(c, p):
                        pool.wait_ge(rinv_ready, c.pair + p)
                        pool.sem_inc(pool_passed, 1)
                        pool.tensor_copy(rx[:, :, :, :], rinv[:, (p - 1) % 2, :, :].rearrange("p h q -> p q h")
                                         .unsqueeze(3).to_broadcast([128, QT, 2, HD])).then_inc(rx_ready, 1)
                    if not rest:
                        continue
                    if s == SELF_DONE:
                        norm_factor(c.norm, rb, EPS)
                    if s == NORM1:
                        add_bias(c.norm, rb, rg * 3 + 1)
                    for j in range(QT):
                        if s == CROSS[j] + CROSS_SUM:
                            pool.wait_ge(x_inv, (rg * 2 + rb) * QT + j + 1)
                            pool.tensor_tensor(XB[:, j, :, :], XB[:, j, :, :],
                                               xinv[:, j, :].unsqueeze(2).to_broadcast([128, H, SK]),
                                               ALU.mult).then_inc(x_norm, 1)
                    for j in range(QT):
                        if s == CROSS[j]:
                            pool.wait_ge(x_max, (rg * 2 + rb) * QT + j + 1)
                            pool.tensor_tensor(XB[:, j, :, :], XB[:, j, :, :],
                                               xmax[:, j, :].unsqueeze(2).to_broadcast([128, H, SK]),
                                               ALU.subtract).then_inc(x_sub, 1)
                    if s == CROSS_DONE:
                        norm_factor(c.norm + 1, rb, EPS)
                    if s == NORM2:
                        add_bias(c.norm + 1, rb, rg * 3 + 2)
                    if s == FF_DONE and more:
                        norm_factor(c.norm + 2, rb, EPS)
                    if s == NORM0 and more:
                        add_bias(c.norm + 2, rb, rg * 3 + 3)

            pool.wait_ge(ld_rows, 16)
            for k in range(2):
                if k:
                    for b in range(B):
                        norm_factor(6 * NL + b, b, EPS2)
                for b in range(B):
                    e = k * (2 + 6 * NL) + b
                    norm_factor(e, b, EPS)
                    add_bias(e, b, k * NL * 3)
                each_half(pool, k, half)

        @block.vector
        def _(dve):
            n1 = 0

            def stage1(ins):
                nonlocal n1
                n1 += 1
                ins.then_inc(dve1, 1)

            def read_T(dst):
                for b in range(B):
                    stage1(dve.tensor_copy(dst[:, b, :], flat(TR[b][:, :, :])))

            def queries_keys_values(cols_, v_stage):
                for b in range(B):
                    stage1(dve.tensor_scalar(q0T[:, b, :], SC[b][:, :], cols_[:, 0:1], None, ALU.add))
                stage1(dve.tensor_scalar(k0T[:, :], X[:, 0:B * SK], cols_[:, 1:2], None, ALU.add))
                v_stage()

            dve.wait_ge(pe1, 1)
            stage1(dve.tensor_copy(ctxT[:, :], X[0:DK, 0:B * SK]))
            read_T(xT)
            dve.wait_ge(pe1, 2)
            dve.wait_ge(ld_w0, 64)
            queries_keys_values(cols0_sb, lambda: stage1(
                dve.tensor_tensor(v0[:, :], O[0:B * SK, 0:D], rows0_sb[0:B * SK, 0, :], ALU.add)))
            dve.wait_ge(pe1, 3)
            scores0 = X[:, 0:NT * SK].rearrange("p (j m) -> p j m", j=NT)
            stage1(dve.tensor_reduce(m0[:, :], scores0, AX.X, ALU.max))
            dve.wait_ge(dve1, 8)
            stage1(dve.tensor_tensor(s0[:, :, :], scores0,
                                     m0[:, :].unsqueeze(2).to_broadcast([128, NT, SK]), ALU.subtract))
            dve.wait_ge(act1, 1)
            stage1(dve.tensor_reduce(z0[:, :], s0[:, :, :], AX.X, ALU.add))
            dve.wait_ge(dve1, 10)
            stage1(dve.reciprocal(m0[:, :], z0[:, :]))
            dve.wait_ge(dve1, 11)
            dve.wait_ge(bd_zero, 4)
            for b in range(B):
                stage1(dve.tensor_tensor(p0[:, QT * b:QT * b + QT, SK * b:SK * b + SK], tiles(s0, b),
                                         m0[:, QT * b:QT * b + QT].unsqueeze(2).to_broadcast([128, QT, SK]),
                                         ALU.mult))
            dve.wait_ge(pe1, 4)
            for b in range(B):
                stage1(dve.tensor_copy(p0T[:, b, :], flat(TR[b][0:B * SK, :, :])))
            dve.wait_ge(pe1, 5)
            for b in range(B):
                stage1(dve.tensor_copy(a0T[:, b, :], SC[b][:, :]))
            stage1(dve.tensor_tensor(t[:, :, :], t[:, :, :], rows0_sb[:, 1:2, :].to_broadcast([128, NT, D]),
                                     ALU.add))
            dve.wait_ge(dve1, 18)
            dve.wait_ge(pe1, 6)
            for b in range(B):
                dve.tensor_tensor(tiles(t, b), ACC[b][:, :, :], tiles(t, b), ALU.add).then_inc(res_ready[b], 1)
            dve.wait_ge(ld_mask, 32)
            dve.tensor_scalar(cap[:, :, :], cap[:, :, :].bitcast(I32), 0, MASKED, ALU.is_equal, ALU.mult).then_inc(cap_ready, 1)
            dve.tensor_scalar(ccap[:, :, :], cm_sb[:, :, :], 0, MASKED, ALU.is_equal, ALU.mult).then_inc(cap_ready, 1)

            def statistics(e, b, res):
                dve.wait_ge(res_ready[b], res)
                for j in range(QT * b, QT * b + QT):
                    ins = dve.bn_stats(stats[:, j, :], t[:, j, :])
                ins.then_inc(ln_stats, 1)
                dve.wait_ge(ln_stats, e + 1)
                dve.sem_inc(dve_passed, 1)
                for j in range(QT * b, QT * b + QT):
                    ins = dve.bn_aggr(mv[:, j, :], stats[:, j, :])
                ins.then_inc(ln_mv, 1)

            def norm_tiles(e, b):
                dve.wait_ge(ln_rstd, e + 1)
                for j in range(QT * b, QT * b + QT):
                    ins = dve.tensor_scalar(xhat[:, j, :], t[:, j, :], mv[:, j, 0:1], rstd[:, j:j + 1],
                                            ALU.subtract, ALU.mult)
                ins.then_inc(ln_xhat, 1)

            def residual(b, sub):
                dve.wait_ge(bias_added[b], sub + 1)
                dve.tensor_tensor(tiles(t, b), ACC[b][:, :, :], tiles(t, b), ALU.add).then_inc(res_ready[b], 1)

            def low(dst, full, hi, split):
                dve.wait_ge(split_hi, split + 1)
                dve.tensor_tensor(dst, full, hi.bitcast(F32), ALU.subtract).then_inc(fill_read, 1)

            def low_A(p, split):
                low(flat(Al[:, p % NP, :, :]), X[:, 0:2 * D], flat(Ah[:, p % NP, :, :]), split)

            def low_H(p, h, split):
                low(Hl[:, p % 2, h, :], X[:, :], Hh[:, p % 2, h, :], split)

            def low_tn(b, g):
                dve.wait_ge(tn_high[b], g + 1)
                dve.tensor_tensor(tnl[:, b, :], tnT[:, b, :], tnh[:, b, :].bitcast(F32),
                                  ALU.subtract).then_inc(tn_low[b], 1)

            def half(c):
                carry, own, rest, more = c.kind
                b, rb, rg, k = c.b, c.rb, c.rg, c.k
                for s in range(STEPS):
                    p, q = divmod(s, QT)
                    n = c.step + s
                    for h in range(2 * own):
                        dve.wait_ge(scored[h], n + 1)
                        if carry or s >= 2:
                            dve.wait_ge(expd[h], n - 1)
                        dve.sem_inc(dve_passed, 1)
                        dve.tensor_tensor_reduce(Ms[:, s % 2, h, :], SC[h][:, :], cap[:, b * QT + q, :], -SCALE,
                                                 3.0e38, ALU.add, ALU.min,
                                                 nmax[:, s % 2, h:h + 1]).then_inc(capped[h], 1)
                    slot(c, s, 0)
                    if q == 0 and before(c, p):
                        for h in range(2):
                            dve.wait_ge(expd[h], n)
                        dve.reciprocal(rinv[:, (p - 1) % 2, :, :],
                                       rsum[:, (p - 1) % 2, :, :]).then_inc(rinv_ready, 1)
                    if (s > 0 and own) or (s == 0 and carry):
                        dve.wait_ge(turned[1], n)
                        if carry or s >= 3:
                            dve.wait_ge(pv_done, n - 2)
                        dve.tensor_copy(PT[:, (s - 1) % 2, 1, :, :], TR[1][:, :, :]).then_inc(pt_ready[1], 1)
                    if rest:
                        rest_of_layer(c, s)
                    slot(c, s, 1)
                    if q == 1 and before(c, p):
                        dve.wait_ge(pv_done, n - 1)
                        dve.wait_ge(fill_read, FREE + c.fill(f"R{p - 1}") + 1)
                        dve.tensor_tensor(OT[:, :], O[:, :], Rsb[:, :], ALU.mult).then_inc(ot_ready, 1)
                    slot(c, s, 2)

            def slot(c, s, i):
                name = c.slots.get((s, i), " ")
                rb = c.rb
                f = c.fill(name) if name != " " else None
                if name[0] == "A":
                    low_A(int(name[1]), c.split(name))
                if name[0] == "H":
                    low_H(int(name[1]), int(name[2]), c.split(name))
                if name[0] == "S":
                    j = int(name[1])
                    dve.wait_ge(fill, f + 1)
                    dve.tensor_tensor(XB[:, j, :, :], X[:, :].rearrange("p (h m) -> p h m", h=H),
                                      ccap[:, rb:rb + 1, :].to_broadcast([128, H, SK]),
                                      ALU.add).then_inc(fill_read, 1)
                    dve.wait_ge(fill_read, FREE + f + 1)
                    dve.tensor_reduce(xmax[:, j, :], XB[:, j, :, :], AX.X, ALU.max).then_inc(x_max, 1)
                if name[0] == "F" and int(name[1]) % 2:
                    m = int(name[1])
                    dve.wait_ge(fill, f + 1)
                    dve.tensor_scalar(hT[:, m, :], X[:, :], cols_sb[:, 2 + m:3 + m], 0.0,
                                      ALU.add, ALU.max).then_inc(fill_read, 1)

            def rest_of_layer(c, s):
                rb, rg, k, more = c.rb, c.rg, c.k, c.kind[3]
                tile = (rg * 2 + rb) * QT
                if s == SELF_DONE:
                    dve.wait_ge(projected, (rg * 2 + rb + 1) * NP)
                    residual(rb, rg * 3)
                    statistics(c.norm, rb, rg * 3 + 2 + k)
                if s == NORM1:
                    norm_tiles(c.norm, rb)
                for j in range(QT):
                    if s == CROSS[j] + CROSS_SUM:
                        dve.wait_ge(x_exp, tile + j + 1)
                        dve.tensor_reduce(xsum[:, j, :], XB[:, j, :, :], AX.X, ALU.add).then_inc(x_sum, 1)
                        dve.wait_ge(x_sum, tile + j + 1)
                        dve.reciprocal(xinv[:, j, :], xsum[:, j, :]).then_inc(x_inv, 1)
                if s == CROSS_DONE:
                    dve.wait_ge(x_out, tile + QT)
                    residual(rb, rg * 3 + 1)
                    statistics(c.norm + 1, rb, rg * 3 + 3 + k)
                if s == NORM2:
                    norm_tiles(c.norm + 1, rb)
                if s == FF_DONE:
                    dve.wait_ge(ff_out, FREE + rg * 2 + rb + 1)
                    residual(rb, rg * 3 + 2)
                    if more:
                        statistics(c.norm + 2, rb, rg * 3 + 4 + k)
                if s == NORM0 and more:
                    norm_tiles(c.norm + 2, rb)
                if s == SPLIT0 and more:
                    low_tn(rb, rg + 1)

            for k in range(2):
                g0 = k * NL
                if k:
                    base = n1
                    dve.wait_ge(pe1, 7)
                    read_T(xT)
                    dve.wait_ge(pe1, 8)
                    dve.wait_ge(ld_w2, 80)
                    queries_keys_values(cols2_sb, lambda: [stage1(dve.tensor_tensor(
                        v2[SK * b:SK * b + SK, b, :], O[SK * b:SK * b + SK, 0:D],
                        rows2_sb[SK * b:SK * b + SK, 0, :], ALU.add)) for b in range(B)])
                    dve.wait_ge(pe1, 9)
                    stage1(dve.tensor_reduce(m2[:, :], X[0:B * SK, :], AX.X, ALU.max))
                    dve.wait_ge(dve1, base + 8)
                    stage1(dve.tensor_scalar(m2[:, :], m2[:, :], -SCALE1, None, ALU.mult))
                    dve.wait_ge(act1, 2)
                    stage1(dve.reciprocal(m2[:, :], z2[:, :]))
                    dve.wait_ge(dve1, base + 10)
                    stage1(dve.tensor_scalar(p2[:, :], p2[:, :], m2[:, 0:1], None, ALU.mult))
                    dve.wait_ge(pe1, 10)
                    for b in range(B):
                        stage1(dve.tensor_tensor(tiles(t, b), ACC[b][:, :, :], tiles(t, b), ALU.add))
                    dve.wait_ge(dve1, base + 13)
                    for b in range(B):
                        statistics(6 * NL + b, b, 1 + 3 * NL)
                        norm_tiles(6 * NL + b, b)
                    dve.wait_ge(ln_xhat, 6 * NL + 2)
                    stage1(dve.tensor_tensor(xhat[:, :, :], xhat[:, :, :],
                                             rows2_sb[:, 1:2, :].to_broadcast([128, NT, D]), ALU.mult))
                    dve.wait_ge(dve1, base + 14)
                    for b in range(B):
                        dve.tensor_tensor(tiles(t, b), tiles(xhat, b), rows2_sb[:, 2:3, :].to_broadcast([128, QT, D]),
                                          ALU.add).then_inc(res_ready[b], 1)
                e = k * (2 + 6 * NL)
                for b in range(B):
                    statistics(e + b, b, g0 * 3 + 1 + k)
                    norm_tiles(e + b, b)
                first = Count(k, 0, 0, FIRST).split("A1") - 3
                low_A(0, first)
                low_tn(0, g0)
                for h in range(2):
                    low_H(0, h, first + 1 + h)
                low_tn(1, g0)
                each_half(dve, k, half)

        @block.scalar
        def _(act):
            act.wait_ge(dve1, 9)
            act.activation(s0[:, :, :], s0[:, :, :], ACT.Exp, scale=SCALE1).then_inc(act1, 1)

            def high(dst, src, f):
                act.wait_ge(fill, f + 1)
                act.activation(dst, src, ACT.Copy).then_inc(split_hi, 1)

            def high_A(p, f):
                high(flat(Ah[:, p % NP, :, :]), X[:, 0:2 * D], f)

            def high_H(p, h, f):
                high(Hh[:, p % 2, h, :], X[:, :], f)

            def normed(b, f, scale, bias):
                act.wait_ge(fill, f + 1)
                act.activation(tnT[:, b, :], X[:, :], ACT.Identity, scale=scale,
                               bias=bias).then_inc(fill_read, 1)

            def normed_high(b, f, k):
                normed(b, f, norm_sb[:, k, 0:1], norm_sb[:, k, 1:2])
                act.wait_ge(fill_read, FREE + f + 1)
                act.activation(tnh[:, b, :], tnT[:, b, :], ACT.Copy).then_inc(tn_high[b], 1)

            def fold_out(name, f):
                act.wait_ge(fill, f + 1)
                if name in "KU":
                    for h in range(2):
                        bd = KBD if name == "K" else VBD
                        ins = act.activation(bd[HD * h:HD * h + HD, :, :, h, :], X[HD * h:HD * h + HD, :]
                                             .rearrange("p (n b m) -> p n b m", n=NP, b=B), ACT.Copy)
                elif name[0] == "M":
                    a = int(name[1])
                    ins = act.activation(Mw[:, :, a * 256:a * 256 + 256].rearrange("p b (n m) -> p n b m", n=4),
                                         X[:, :].rearrange("p (n b m) -> p n b m", n=4, b=B), ACT.Copy)
                else:
                    ins = act.activation(flat(Nw[:, int(name[1]), :, :]), X[:, :], ACT.Copy)
                ins.then_inc(fill_read, 1)

            def half(c):
                carry, own, rest, more = c.kind
                for s in range(STEPS):
                    p, q = divmod(s, QT)
                    n = c.step + s
                    for h in range(2):
                        if own:
                            act.wait_ge(capped[h], FREE + n + 1)
                            if carry or s >= 2:
                                act.wait_ge(turned[h], n - 1)
                            act.activation(E[:, s % 2, h, :], Ms[:, s % 2, h, :], ACT.Exp, scale=-1.0,
                                           bias=nmax[:, s % 2, h:h + 1],
                                           accum_out=rsum[:, p % 2, h, q:q + 1]).then_inc(expd[h], 1)
                        if h == 0:
                            slot(c, s, 0)
                    if (s > 0 and own) or (s == 0 and carry):
                        act.wait_ge(turned[0], n)
                        if carry or s >= 3:
                            act.wait_ge(pv_done, n - 2)
                        act.activation(PT[:, (s - 1) % 2, 0, :, :], TR[0][:, :, :], ACT.Copy).then_inc(pt_ready[0], 1)
                    if rest:
                        rest_of_layer(c, s)
                    slot(c, s, 1)
                    slot(c, s, 2)

            def slot(c, s, i):
                name = c.slots.get((s, i), " ")
                rb, rg, k = c.rb, c.rg, c.k
                f = c.fill(name) if name != " " else None
                if name[0] == "V":
                    act.wait_ge(fill, f + 1)
                    act.activation(flat(V[:, int(name[1]) % 2, :, :]), X[:, :], ACT.Copy).then_inc(fill_read, 1)
                if name[0] == "A":
                    high_A(int(name[1]), f)
                if name[0] == "H":
                    high_H(int(name[1]), int(name[2]), f)
                if name[0] == "R":
                    act.wait_ge(fill, f + 1)
                    act.activation(Rsb[:, :], X[:, :], ACT.Copy).then_inc(fill_read, 1)
                if name == "T1":
                    normed(rb, f, norm_sb[:, k, 0:1], norm_sb[:, k, 1:2])
                if name == "T2":
                    act.wait_ge(ld_ff, (rg + 1) * 32)
                    normed(rb, f, cols_sb[:, 0:1], cols_sb[:, 1:2])
                if name == "T0":
                    normed_high(rb, f, k)
                if name[0] == "P":
                    j = int(name[1])
                    act.wait_ge(fill, f + 1)
                    if j >= 2:
                        act.wait_ge(x_out, (rg * 2 + rb) * QT + j - 1)
                    act.activation(flat(PX[:, j % 2, :, :]), X[:, :], ACT.Copy).then_inc(fill_read, 1)
                if name[0] == "F" and int(name[1]) % 2 == 0:
                    m = int(name[1])
                    act.wait_ge(fill, f + 1)
                    act.activation(hT[:, m, :], X[:, :], ACT.Relu,
                                   bias=cols_sb[:, 2 + m:3 + m]).then_inc(fill_read, 1)
                if name in FOLD:
                    fold_out(name, f)

            def rest_of_layer(c, s):
                for j in range(QT):
                    if s == CROSS[j] + CROSS_EXP:
                        act.wait_ge(x_sub, (c.rg * 2 + c.rb) * QT + j + 1)
                        act.activation(XB[:, j, :, :], XB[:, j, :, :], ACT.Exp, scale=SCALE).then_inc(x_exp, 1)

            for k in range(2):
                if k:
                    act.wait_ge(dve1, 18 + 9)
                    act.activation(p2[:, :], X[0:B * SK, :], ACT.Exp, scale=SCALE1, bias=m2[:, 0:1],
                                   accum_out=z2[:, 0:1]).then_inc(act1, 1)
                at = Count(k, 0, 0, FIRST).entry
                if k == 0:
                    act.wait_ge(ld_w2, 80)
                for f, name in enumerate(ENTRY):
                    if name == "A0":
                        high_A(0, at + f)
                    elif name[0] == "T":
                        normed_high(int(name[2]), at + f, k)
                    elif name[0] == "H":
                        high_H(0, int(name[2]), at + f)
                    else:
                        if name == "K":
                            act.wait_ge(bd_zero, 4)
                        fold_out(name, at + f)
                each_half(act, k, half)

        @block.tensor
        def _(pe):
            for free in (*capped, *pt_ready, fill_read):
                pe.sem_inc(free, FREE)

            def three(out_, wh, wl, mh, ml):
                pe.matmul(out_, wh, ml, start=True, stop=False)
                pe.matmul(out_, wl, mh, start=False, stop=False)
                return pe.matmul(out_, wh, mh, start=False, stop=True)

            def turn_tokens(src):
                for b in range(B):
                    for q in range(QT):
                        ins = pe.transpose(TR[b][:, q, :], src[:, QT * b + q, :], ident[:, :])
                return ins

            def queries_keys_values(w, wkv):
                for b in range(B):
                    pe.matmul(SC[b][:, :], w[:, 0, :], xT[:, b, :], start=True, stop=True)
                pe.matmul(X[:, 0:B * SK], wkv[:, 0, :], ctxT[:, :], start=True, stop=True)
                return pe.matmul(O[0:B * SK, 0:D], ctxT[:, :], wkv[:, 1, :], start=True, stop=True)

            pe.wait_ge(const_ready, 3)
            pe.wait_ge(ld_in, 32)
            pe.transpose(X[0:DK, 0:B * SK], ctx_sb[:, :], ident[0:B * SK, 0:B * SK])
            turn_tokens(t).then_inc(pe1, 1)
            pe.wait_ge(dve1, 3)
            pe.wait_ge(ld_w0, 64)
            queries_keys_values(w0_sb, w0kv_sb).then_inc(pe1, 1)
            pe.wait_ge(dve1, 7)
            for j in range(NT):
                b, q = divmod(j, QT)
                mm = pe.matmul(X[:, j * SK:j * SK + SK], q0T[:, b, q * 128:q * 128 + 128],
                               k0T[:, b * SK:b * SK + SK], start=True, stop=True)
            mm.then_inc(pe1, 1)
            pe.wait_ge(dve1, 13)
            for j in range(NT):
                b, q = divmod(j, QT)
                mm = pe.transpose(TR[b][0:B * SK, q, :], p0[:, j, :], ident[:, :])
            mm.then_inc(pe1, 1)
            pe.wait_ge(dve1, 15)
            for b in range(B):
                mm = pe.matmul(SC[b][:, :], v0[:, :], p0T[:, b, :], start=True, stop=True)
            mm.then_inc(pe1, 1)
            pe.wait_ge(dve1, 17)
            for j in range(NT):
                b, q = divmod(j, QT)
                mm = pe.matmul(ACC[b][:, q, :], a0T[:, b, q * 128:q * 128 + 128], w0_sb[:, 1, :],
                               start=True, stop=True)
            mm.then_inc(pe1, 1)

            def turn_normed(f, e, b):
                pe.wait_ge(fill_read, FREE + f)
                pe.wait_ge(ln_xhat, e + 1)
                for q in range(QT):
                    ins = pe.transpose(X[:, q * 128:q * 128 + 128], xhat[:, QT * b + q, :], ident[:, :])
                ins.then_inc(fill, 1)

            def fold_qk(g, f, p):
                if p % NP == 0:
                    pe.wait_ge(ld_wqk, (g + 1) * 16)
                pe.wait_ge(fill_read, FREE + f)
                for h in range(2):
                    mm = pe.matmul(X[:, h * D:h * D + D], wqk_sb[:, p % NP, 1, h, :], wqk_sb[:, p % NP, 0, h, :],
                                   start=True, stop=True)
                mm.then_inc(fill, 1)

            def keys(f, b, p, h):
                pe.wait_ge(fill_read, FREE + f)
                three(X[:, :], Ah[:, p % NP, h, :], Al[:, p % NP, h, :], tnh[:, b, :],
                      tnl[:, b, :]).then_inc(fill, 1)

            def fold_context(name, f, g):
                pe.wait_ge(fill_read, FREE + f)
                if name == "K":
                    pe.wait_ge(ld_c, (g + 1) * 32)
                if name in "KU":
                    for n in range(NP):
                        mm = pe.matmul(X[:, n * 64:n * 64 + 64], ckv_sb[:, "KU".index(name), n, :], ctxT[:, :],
                                       start=True, stop=True)
                elif name[0] == "M":
                    for m in range(4):
                        n = int(name[1]) * 4 + m
                        mm = pe.matmul(X[:, m * 128:m * 128 + 128], cqo_sb[:, 0, n, :],
                                       KBD[:, n, :, :, :].rearrange("p b h m -> p (b h m)"), start=True, stop=True)
                else:
                    for n in range(NP):
                        mm = pe.matmul(X[64 * (n % 2):64 * (n % 2) + 64, (n // 2) * D:(n // 2) * D + D],
                                       VBD[:, n, int(name[1]), :, :].rearrange("p h m -> p (h m)"),
                                       cqo_sb[:, 1, n, :], start=True, stop=True)
                mm.then_inc(fill, 1)

            def half(c):
                carry, own, rest, more = c.kind
                g, b = c.g, c.b
                for s in range(STEPS):
                    p, q = divmod(s, QT)
                    n = c.step + s
                    for h in range(2 * own):
                        pe.wait_ge(capped[h], FREE + n)
                        if s == 0:
                            pe.wait_ge(tn_low[b], g + 1)
                        if q == 0:
                            pe.wait_ge(fill_read, FREE + (c.fill(f"H{p}{h}") + 1 if p else c.fill("V0")))
                        three(SC[h][:, :], tnh[:, b, q * 128:q * 128 + 128], tnl[:, b, q * 128:q * 128 + 128],
                              Hh[:, p % 2, h, :], Hl[:, p % 2, h, :]).then_inc(scored[h], 1)
                    slot(c, s, 0)
                    if (s > 0 and own) or (s == 0 and carry):
                        for h in range(2):
                            pe.wait_ge(expd[h], n)
                            pe.wait_ge(pt_ready[h], FREE + n - 1)
                            for m in range(KT):
                                mm = pe.transpose(TR[h][:, m, :], E[:, (s - 1) % 2, h, m * 128:m * 128 + 128],
                                                  ident[:, :])
                            mm.then_inc(turned[h], 1)
                    if rest:
                        rest_of_layer(c, s)
                    slot(c, s, 1)
                    if q == 2 and before(c, p):
                        pb = b if p > 0 else 1 - b
                        lp = (p - 1) % NP
                        pe.wait_ge(ot_ready, c.pair + p)
                        for m in range(QT):
                            mm = pe.matmul(ACC[pb][:, m, :], OT[:, m * 128:m * 128 + 128], wvo_sb[:, lp, 1, :],
                                           start=(lp == 0 and m == 0), stop=(lp == NP - 1), skip_group_check=True)
                        mm.then_inc(projected, 1)
                    if (own and s >= 2) or (carry and s < 2):
                        times_v(c, s)
                    slot(c, s, 2)

            def slot(c, s, i):
                name = c.slots.get((s, i), " ")
                if name == " ":
                    return
                f = c.fill(name)
                rb, rg, b, g = c.rb, c.rg, c.b, c.g
                p = s // QT
                if name[0] == "V":
                    pe.wait_ge(ld_wvo, (g * NP + p + 1) * 16)
                    pe.wait_ge(fill_read, FREE + f)
                    for m in range(KT):
                        mm = pe.matmul(X[:, m * 128:m * 128 + 128], tnT[:, b, m * 128:m * 128 + 128],
                                       wvo_sb[:, p, 0, :], start=True, stop=True)
                    mm.then_inc(fill, 1)
                if name[0] == "A":
                    fold_qk(g + b, f, p + 1)
                if name[0] == "H":
                    nb = b if p < NP - 1 else 1 - b
                    if p == NP - 1:
                        pe.wait_ge(tn_low[nb], g + b + 1)
                    keys(f, nb, p + 1, int(name[2]))
                if name[0] == "R":
                    pe.wait_ge(rx_ready, c.pair + p)
                    pe.wait_ge(fill_read, FREE + f)
                    for m in range(QT):
                        mm = pe.transpose(X[:, m * 128:m * 128 + 128],
                                          rx[:, m, :, :].rearrange("p h d -> p (h d)"), ident[:, :])
                    mm.then_inc(fill, 1)
                if name[0] == "T":
                    turn_normed(f, c.norm + {"T1": 0, "T2": 1, "T0": 2}[name], rb)
                if name[0] == "S":
                    j = int(name[1])
                    pe.wait_ge(fill_read, FREE + f)
                    pe.matmul(X[:, :], tnT[:, rb, j * 128:j * 128 + 128], Mw[:, rb, :], start=True,
                              stop=True).then_inc(fill, 1)
                if name[0] == "P":
                    j = int(name[1])
                    pe.wait_ge(x_norm, (rg * 2 + rb) * QT + j + 1)
                    pe.wait_ge(fill_read, FREE + f)
                    xb = XB[:, j, :, :].rearrange("p h m -> p (h m)")
                    for m in range(4):
                        mm = pe.transpose(X[:, m * 128:m * 128 + 128], xb[:, m * 128:m * 128 + 128], ident[:, :])
                    mm.then_inc(fill, 1)
                if name[0] == "F":
                    m = int(name[1])
                    if m == 0:
                        pe.wait_ge(ld_ff, (rg + 1) * 32)
                    pe.wait_ge(fill_read, FREE + f)
                    pe.matmul(X[:, :], ffw_sb[:, 0, m * 128:m * 128 + 128], tnT[:, rb, :], start=True,
                              stop=True).then_inc(fill, 1)
                if name in FOLD:
                    fold_context(name, f, g)

            def times_v(c, s):
                n = c.step + s - 2
                p, q = divmod(s - 2, QT)
                if q == 0 and (p > 0 or c.kind[0]):
                    pe.wait_ge(ot_ready, c.pair + p)
                for h in range(2):
                    pe.wait_ge(pt_ready[h], FREE + n + 1)
                for m in range(KT):
                    for h in range(2):
                        mm = pe.matmul(O[HD * h:HD * h + HD, q * 128:q * 128 + 128],
                                       V[:, p % 2, m, HD * h:HD * h + HD], PT[:, s % 2, h, m, :],
                                       start=(m == 0), stop=(m == KT - 1))
                mm.then_inc(pv_done, 1)

            def rest_of_layer(c, s):
                rb, rg = c.rb, c.rg
                for j in range(QT):
                    if s == CROSS_OUT[j]:
                        pe.wait_ge(fill_read, FREE + c.fill(f"P{j}") + 1)
                        for m in range(4):
                            mm = pe.matmul(ACC[rb][:, j, :], PX[:, j % 2, m, :], Nw[:, rb, m, :],
                                           start=(m == 0), stop=(m == 3))
                        mm.then_inc(x_out, 1)
                if s == FF_OUT:
                    pe.wait_ge(fill_read, FREE + c.fill(f"F{NF - 1}") + 1)
                if 0 <= s - FF_OUT < 2:
                    for q in range(2 * (s - FF_OUT), 2 * (s - FF_OUT) + 2):
                        for m in range(NF):
                            mm = pe.matmul(ACC[rb][:, q, :], hT[:, m, q * 128:q * 128 + 128],
                                           ffw_sb[:, 1, m * 128:m * 128 + 128], start=(m == 0), stop=(m == NF - 1))
                    if s == FF_OUT + 1:
                        mm.then_inc(ff_out, 1)

            for k in range(2):
                if k:
                    d1 = 18
                    for b in range(B):
                        pe.wait_ge(res_ready[b], 1 + 3 * NL)
                    pe.wait_ge(ld_w2, 80)
                    turn_tokens(t).then_inc(pe1, 1)
                    pe.wait_ge(dve1, d1 + 2)
                    queries_keys_values(w2_sb, w2kv_sb).then_inc(pe1, 1)
                    pe.wait_ge(dve1, d1 + 7)
                    for b in range(B):
                        mm = pe.matmul(X[SK * b:SK * b + SK, :], k0T[:, SK * b:SK * b + SK], q0T[:, b, :],
                                       start=True, stop=True)
                    mm.then_inc(pe1, 1)
                    pe.wait_ge(dve1, d1 + 11)
                    for j in range(NT):
                        b, q = divmod(j, QT)
                        mm = pe.matmul(ACC[b][:, q, :], p2[:, q * 128:q * 128 + 128], v2[:, b, :],
                                       start=True, stop=True)
                    mm.then_inc(pe1, 1)
                g0 = k * NL
                at = Count(k, 0, 0, FIRST).entry
                for f, name in enumerate(ENTRY):
                    if name == "A0":
                        fold_qk(g0, at + f, 0)
                    elif name[0] == "T":
                        turn_normed(at + f, k * (2 + 6 * NL) + int(name[2]), int(name[2]))
                    elif name[0] == "H":
                        if name == "H00":
                            pe.wait_ge(tn_low[0], g0 + 1)
                        keys(at + f, 0, 0, int(name[2]))
                    else:
                        fold_context(name, at + f, g0)
                each_half(pe, k, half)


def kernel(**inputs):
    import numpy as np
    import concourse.bacc as bacc
    from concourse.bass_utils import run_bass_kernel_spmd

    a = {k: np.asarray(v) for k, v in inputs.items()}
    stacks = ("L1_xattn_", "L3_xattn_")

    def both(name):
        return np.concatenate([a[s + name] for s in stacks])

    G = 2 * NL
    wqT = both("sa_q").transpose(0, 2, 1).reshape(G, NP, 2, HD, D)
    wkT = both("sa_kv")[:, :, :H * HD].transpose(0, 2, 1).reshape(G, NP, 2, HD, D)
    wv = both("sa_kv")[:, :, H * HD:].reshape(G, D, NP, 128).transpose(0, 2, 1, 3).reshape(G * NP, D, 128)
    wo = both("sa_ow").reshape(G * NP, 128, D)
    cqT = both("ca_q").transpose(0, 2, 1).reshape(G, NP, 128, D)
    co = both("ca_ow").reshape(G, NP, 128, D)
    w2f = both("ff_w2").reshape(G, NF, 128, D).transpose(0, 2, 1, 3).reshape(G, 128, NF * D)
    arrays = {
        "x": a["x"], "ctx": a["ctx_512"], "mask": a["mask_BxSxS_ik0"], "cmask": a["mask_Bx1xS2_if1"],
        "w0": np.stack([a["L0_xattn_Wq"], a["L0_xattn_Wo"]], 1),
        "w0kv": np.stack([a["L0_xattn_Wk"], a["L0_xattn_Wv"]], 1),
        "w2": a["L2_xattn_Wq"][:, None, :],
        "w2kv": np.stack([a["L2_xattn_Wk"], a["L2_xattn_Wv"]], 1),
        "rows0": np.stack([a["L0_xattn_bv"], a["L0_xattn_bo"]]),
        "rows2": np.stack([a["L2_xattn_bv"], a["L2_xattn_gamma"], a["L2_xattn_beta"]]),
        "cols0": np.stack([a["L0_xattn_bq"], a["L0_xattn_bk"]], 1),
        "cols2": np.stack([a["L2_xattn_bq"], a["L2_xattn_bk"]], 1),
        "wqk": np.stack([wqT, wkT], 2).transpose(0, 4, 1, 2, 3, 5), "wvo": np.stack([wv, wo], 2),
        "ckv": both("ca_kv").reshape(G, DK, 2, NP, 128),
        "cqo": np.stack([cqT, co], 1).transpose(0, 3, 1, 2, 4),
        "ffw": np.stack([both("ff_w1"), w2f], 2),
        "cols": np.concatenate([both("pre_g")[:, :, None], both("pre_b")[:, :, None],
                                both("ff_b1").reshape(G, NF, 128).transpose(0, 2, 1)], 2),
        "rows": np.stack([both("sa_ob"), both("ca_ob"), both("ff_b2")], 1),
        "norms": np.stack([np.stack([a[s + "norm_g"], a[s + "norm_b"]], 1) for s in stacks], 1),
    }
    arrays = {k: np.ascontiguousarray(v) for k, v in arrays.items()}
    nc = bacc.Bacc("TRN2", target_bir_lowering=False, num_devices=1)
    aps = {k: nc.dram_tensor(k, v.shape, mybir.dt.from_np(v.dtype), kind="ExternalInput").ap()
           for k, v in arrays.items()}
    out = nc.dram_tensor("out", (B, S, D), F32, kind="ExternalOutput").ap()
    build(nc, out=out, **aps)
    r = run_bass_kernel_spmd(nc, [arrays], core_ids=[0])
    return r.results[0]["out"]
```

```python
from contextlib import ExitStack

import concourse.bass as bass
from concourse import mybir

F32 = mybir.dt.float32
F32R = mybir.dt.float32r
I32 = mybir.dt.int32
ALU = mybir.AluOpType
ACT = mybir.ActivationFunctionType
AX = mybir.AxisListType

B = 2
S = 512
D = 128
SK = 32
DK = 64
H = 16
HD = 64
NP = H // 2
FF = 512
NL = 6
QT = S // 128
NT = B * QT
KT = S // 128
NF = FF // 128
SCALE = HD ** -0.5
MASKED = -1.0e30
SCALE1 = 128 ** -0.5
EPS = 1e-5
EPS2 = 1e-6

FREE = 1

STEPS = NP * QT

STATS, NORM = 1, 2
SELF_DONE = 2
CROSS = (6, 7, 7, 8)
CROSS_EXP, CROSS_SUM = 1, 2
CROSS_OUT = (11, 12, 12, 13)
CROSS_DONE = 14
FF_OUT = 21
FF_DONE, SPLIT0 = 23, 27

REST = {"T1": (5, 1), "S0": (6, 2), "S1": (7, 0), "S2": (7, 2), "S3": (8, 2),
        "P0": (10, 2), "P1": (11, 0), "P2": (11, 2), "P3": (12, 2),
        "T2": (17, 1), "F0": (18, 2), "F1": (19, 0), "F2": (19, 2), "F3": (20, 2), "T0": (26, 2)}
FOLD = {"K": (22, 2), "U": (23, 0), "M0": (23, 2), "M1": (24, 2), "N0": (27, 0), "N1": (27, 2)}

STATS1, ENTRY1, SPLIT1 = 1, (3, 2), 4

FIRST = (False, True, False, True)
MIDDLE = (True, True, True, True)
LAST = (True, True, True, False)
DRAIN = (True, False, True, False)


def slots(kind, b):
    carry, own, rest, more = kind
    at = {}

    def put(where, name):
        assert where not in at
        at[where] = name

    for p in range(NP):
        s = p * QT
        if own:
            put((s, 0), f"V{p}")
            if p < NP - 1 if b == 0 else p == NP - 1 and more:
                put((s, 1), f"A{p + 1}")
            if p < NP - 1 or more:
                put((s + 1, 2), f"H{p + 1}0")
                put((s + 2, 0), f"H{p + 1}1")
        if (p > 0 or carry) and (own or p == 0):
            put((s + 1, 0), f"R{p - 1}")
    if rest:
        for name, where in REST.items():
            if name != "T0" or more:
                put(where, name)
    if own and b == 0:
        for name, where in FOLD.items():
            put(where, name)
    if kind == FIRST:
        put(ENTRY1, "E")
    return at


def fills(kind, b):
    at = slots(kind, b)
    return [at[where] for where in sorted(at)]


ENTRY = ["A0", "T", "H00", "H01"]


class Count:

    def __init__(self, k, layer, b, kind, trip=0):
        self.k, self.layer = k, layer
        self.g = layer + k * NL
        self.b, self.kind = b, kind
        self.slots = slots(kind, b)
        self.order = fills(kind, b)
        first, odd, even = (len(fills(*x)) for x in ((FIRST, 0), (MIDDLE, 1), (MIDDLE, 0)))
        last, drain = len(fills(LAST, 1)), len(fills(DRAIN, 0))
        stack = len(ENTRY) + first + (NL - 1) * (odd + even) + last + drain
        base = k * stack + len(ENTRY)
        if kind == FIRST:
            self.base = base
        elif kind == MIDDLE:
            self.base = base + first + trip * (odd + even) + (odd if b == 0 else 0)
        else:
            self.base = base + first + (NL - 1) * (odd + even) + (last if kind == DRAIN else 0)
        self.entry = k * stack
        self.rb = 1 - b
        self.rg = self.g if b else self.g - 1
        rests = trip * 2 + (1 if b == 0 else 0) if kind == MIDDLE else 2 * (NL - 1) + (kind == DRAIN)
        if kind == FIRST:
            rests = 0
        self.norm = k * (2 + 6 * NL) + 2 + rests * 3 - (kind == DRAIN)
        self.step = (self.g * 2 + b) * STEPS
        self.pair = (self.g * 2 + b) * NP

    def fill(self, name):
        return self.base + self.order.index(name)

    def split(self, name=None):
        splits = [x for x in self.order if x[0] in "AH"]
        odd, even = (sum(x[0] in "AH" for x in fills(MIDDLE, b)) for b in (1, 0))
        last = sum(x[0] in "AH" for x in fills(LAST, 1))
        stack = 3 + even + (NL - 1) * (odd + even) + last
        before = self.k * stack + 3 + self.layer * (odd + even) + self.b * even
        assert stack % 2 == 0 and (odd + even) % 2 == 0
        return before + (splits.index(name) if name else 0)

    def buffer(self, name):
        splits = [x for x in self.order if x[0] in "AH"]
        even = sum(x[0] in "AH" for x in fills(MIDDLE, 0))
        return (3 + self.b * even + splits.index(name)) % 2


def build(nc, x, ctx, mask, cmask, w0, w0kv, w2, w2kv, rows0, rows2, cols0, cols2, wqk, wvo, ckv, cqo, ffw, cols, first, rows,
          norms, out):
    st = ExitStack()
    with st:
        def sb(name, shape, dt=F32):
            return st.enter_context(nc.sbuf_tensor(name, shape, dt))

        def sem(name):
            return st.enter_context(nc.semaphore(name))

        t = sb("t", [128, NT, D])
        cap = sb("cap", [128, NT, S])
        ccap = sb("ccap", [128, B, SK])
        ident = sb("ident", [128, 128])
        neghalf = sb("neghalf", [128, NT])
        ctx_sb = sb("ctx_sb", [B * SK, DK])
        ctxT = sb("ctxT", [DK, B * SK])
        norm_sb = sb("norm_sb", [128, 2, 2])
        first_sb = sb("first_sb", [128, 2, D])
        rows_sb = sb("rows_sb", [128, 3, D])
        stats = sb("stats", [128, NT, 6])
        mv = sb("mv", [128, NT, 2])
        vpe = sb("vpe", [128, NT])
        rstd = sb("rstd", [128, NT])
        xhat = sb("xhat", [128, NT, D])
        tnT = sb("tnT", [128, B, S])
        tnh = sb("tnh", [128, B, S], F32R)
        tnl = sb("tnl", [128, B, S], F32R)
        wqk_sb = sb("wqk_sb", [HD, NP, 2, 2, D])
        wvo_sb = sb("wvo_sb", [128, NP, 2, 128])
        Ah = sb("Ah", [128, NP, 2, D], F32R)
        Al = sb("Al", [128, NP, 2, D], F32R)
        raw = sb("raw", [128, 2, S])
        Hh = sb("Hh", [128, 2, 2, S], F32R)
        Hl = sb("Hl", [128, 2, 2, S], F32R)
        V = sb("V", [128, 2, KT, 128])
        Ms = sb("Ms", [128, 2, 2, S])
        nmax = sb("nmax", [128, 2, 2])
        E = sb("E", [128, 2, 2, S])
        rsum = sb("rsum", [128, 2, 2, QT])
        rinv = sb("rinv", [128, 2, 2, QT])
        rx = sb("rx", [128, QT, 2, HD])
        PT = sb("PT", [128, 2, 2, KT, 128])
        Rsb = sb("Rsb", [128, S])
        OT = sb("OT", [128, S])
        ckv_sb = sb("ckv_sb", [DK, 2, NP, 128])
        cqo_sb = sb("cqo_sb", [128, 2, NP, D])
        KBD = sb("KBD", [128, NP, B, 2, SK])
        VBD = sb("VBD", [128, NP, B, 2, SK])
        Mw = sb("Mw", [128, B, H * SK])
        Nw = sb("Nw", [128, B, 4, D])
        XB = sb("XB", [128, QT, H, SK])
        xmax = sb("xmax", [128, QT, H])
        xsum = sb("xsum", [128, QT, H])
        xinv = sb("xinv", [128, QT, H])
        PX = sb("PX", [128, 2, 4, 128])
        ffw_sb = sb("ffw_sb", [128, 2, FF])
        cols_sb = sb("cols_sb", [128, 2 + NF])
        hT = sb("hT", [128, NF, S])
        cm_sb = sb("cm_sb", [128, B, SK], I32)
        w0_sb = V[:, 0, 0:2, :]
        w0kv_sb = V[0:DK, 0, 2:4, :]
        w2_sb = V[:, 0, 0:1, :]
        w2kv_sb = V[0:DK, 0, 2:4, :]
        rows0_sb = V[:, 1, 0:2, :]
        rows2_sb = V[:, 1, 0:3, :]
        cols0_sb = sb("cols0_sb", [128, 2])
        cols2_sb = sb("cols2_sb", [128, 2])
        xT = E[:, 0, :, :]
        q0T = E[:, 1, :, :]
        k0T = OT[:, 0:B * SK]
        v0 = OT[0:B * SK, 128:128 + D]
        v2 = hT[0:B * SK, 2, 0:B * D].rearrange("p (b d) -> p b d", b=B)
        s0 = XB[:, 0, :, :].rearrange("p (j i) m -> p j (i m)", j=NT)[:, :, 0:SK]
        p0 = hT[:, 0, :].rearrange("p (j m) -> p j m", j=NT)
        m0 = sb("m0", [128, NT])
        z0 = sb("z0", [128, NT])
        p0T = Ms[0:B * SK, 0, :, :]
        a0T = Ms[:, 1, :, :]
        p2 = hT[0:B * SK, 1, :]
        m2 = sb("m2", [B * SK, 1])
        z2 = sb("z2", [B * SK, 1])

        SC = [st.enter_context(nc.psum_tensor(f"SC{h}", [128, S], F32)) for h in range(2)]
        TR = [st.enter_context(nc.psum_tensor(f"TR{h}", [128, 4, 128], F32)) for h in range(2)]
        O = st.enter_context(nc.psum_tensor("O", [128, S], F32))
        X = st.enter_context(nc.psum_tensor("X", [128, S], F32))
        ACC = [st.enter_context(nc.psum_tensor(f"ACC{b}", [128, QT, D], F32)) for b in range(B)]

        ld_in = sem("ld_in")
        ld_mask = sem("ld_mask")
        ld_w0 = sem("ld_w0")
        ld_w2 = sem("ld_w2")
        const_ready = sem("const_ready")
        cap_ready = sem("cap_ready")
        bd_zero = sem("bd_zero")
        pe1 = sem("pe1_products")
        dve1 = sem("dve1_stages")
        act1 = sem("act1_stages")
        res_ready = [sem(f"res_ready{b}") for b in range(B)]
        bias_added = [sem(f"bias_added{b}") for b in range(B)]
        ln_stats = sem("ln_stats")
        ln_mv = sem("ln_mv")
        ln_vpe = sem("ln_vpe")
        ln_rstd = sem("ln_rstd")
        ln_xhat = sem("ln_xhat")
        tn_high = [sem(f"tn_high{b}") for b in range(B)]
        tn_low = [sem(f"tn_low{b}") for b in range(B)]
        ld_wqk = sem("ld_wqk")
        ld_wvo = sem("ld_wvo")
        ld_c = sem("ld_c")
        ld_ff = sem("ld_ff")
        ld_rows = sem("ld_rows")
        fill = sem("spare_filled")
        fill_read = sem("spare_read")
        split_hi = sem("split_hi")
        split_lo = sem("split_lo")
        scored = [sem(f"scored{h}") for h in range(2)]
        capped = [sem(f"capped{h}") for h in range(2)]
        expd = [sem(f"expd{h}") for h in range(2)]
        turned = [sem(f"turned{h}") for h in range(2)]
        pt_ready = [sem(f"pt_ready{h}") for h in range(2)]
        pv_done = sem("pv_done")
        rinv_ready = sem("rinv_ready")
        rx_ready = sem("rx_ready")
        ot_ready = sem("ot_ready")
        projected = sem("projected")
        x_max = sem("x_max")
        x_sub = sem("x_sub")
        x_exp = sem("x_exp")
        x_sum = sem("x_sum")
        x_inv = sem("x_inv")
        x_norm = sem("x_norm")
        x_out = sem("x_out")
        ff_out = sem("ff_out")
        dve_passed = sem("dve_passed")
        pool_passed = sem("pool_passed")
        stored = sem("stored")

        block = st.enter_context(nc.Block())

        def each_half(eng, k, half):
            half(Count(k, 0, 0, FIRST))
            with eng.Fori(0, NL - 1) as l:
                half(Count(k, l, 1, MIDDLE, l))
                half(Count(k, l + 1, 0, MIDDLE, l))
            half(Count(k, NL - 1, 1, LAST))
            half(Count(k, NL, 0, DRAIN))

        def flat(ap):
            return ap.rearrange("p a d -> p (a d)")

        def tiles(a, b):
            return a[:, QT * b:QT * b + QT, :]

        def before(c, p):
            carry, own, _, _ = c.kind
            return (p > 0 or carry) and (own or p == 0)

        @block.sync
        def _(sp):
            sp.sem_inc(ff_out, FREE)

            def attention_weights(g):
                sp.dma_start(wqk_sb[:, :, :, :, :], wqk[bass.ds(g, 1), :, :, :, :, :]
                             .rearrange("o p n a h d -> (o p) n a h d")).then_inc(ld_wqk, 16)

            def pair_weights(it, p, first=False):
                if not first:
                    sp.wait_ge(ld_wvo, it * 16)
                sp.dma_start(wvo_sb[:, p, :, :], wvo[bass.ds(it, 1), :, :, :]
                             .rearrange("o p a d -> (o p) a d")).then_inc(ld_wvo, 16)

            def cross_weights(g):
                sp.dma_start(ckv_sb[:, :, :, :], ckv[bass.ds(g, 1), :, :, :, :]
                             .rearrange("o p a n d -> (o p) a n d")).then_inc(ld_c, 16)
                sp.dma_start(cqo_sb[:, :, :, :], cqo[bass.ds(g, 1), :, :, :, :]
                             .rearrange("o p a n d -> (o p) a n d")).then_inc(ld_c, 16)

            def ff_weights(g):
                sp.wait_ge(ff_out, FREE + g * 2)
                sp.dma_start(ffw_sb[:, :, :], ffw[bass.ds(g, 1), :, :, :]
                             .rearrange("o p a n -> (o p) a n")).then_inc(ld_ff, 16)
                sp.dma_start(cols_sb[:, :], cols[bass.ds(g, 1), :, :]
                             .rearrange("o p n -> (o p) n")).then_inc(ld_ff, 16)

            def biases(g):
                sp.wait_ge(bias_added[1], g * 3 + 1)
                sp.dma_start(rows_sb[:, :, :], rows[bass.ds(g, 1), :, :].rearrange("o a n -> (o a) n")
                             .partition_broadcast(128)).then_inc(ld_rows, 16)

            sp.dma_start(t[:, :, :], x.rearrange("b (q p) d -> p (b q) d", p=128)).then_inc(ld_in, 16)
            sp.dma_start(ctx_sb[:, :], ctx.rearrange("b m d -> (b m) d")).then_inc(ld_in, 16)
            sp.dma_start(first_sb[:, :, :], first.partition_broadcast(128)).then_inc(ld_rows, 16)
            sp.dma_start(w0_sb[:, :, :], w0).then_inc(ld_w0, 16)
            sp.dma_start(w0kv_sb[:, :, :], w0kv).then_inc(ld_w0, 16)
            sp.dma_start(cols0_sb[:, :], cols0).then_inc(ld_w0, 16)
            sp.dma_start(rows0_sb[:, :, :], rows0.partition_broadcast(128)).then_inc(ld_w0, 16)
            sp.dma_start(norm_sb[:, :, :], norms).then_inc(ld_w0, 16)
            sp.dma_start(cm_sb[:, :, :],
                         cmask.rearrange("b o m -> (b o) m").partition_broadcast(128)).then_inc(ld_mask, 16)
            sp.dma_start(cap[:, :, :].bitcast(I32), mask.rearrange("b (q p) k -> p (b q) k", p=128)).then_inc(ld_mask, 16)
            for k in range(2):
                g0 = k * NL
                if k:
                    sp.wait_ge(pv_done, g0 * 2 * STEPS)
                    sp.dma_start(w2_sb[:, :, :], w2).then_inc(ld_w2, 16)
                    sp.dma_start(w2kv_sb[:, :, :], w2kv).then_inc(ld_w2, 16)
                    sp.dma_start(cols2_sb[:, :], cols2).then_inc(ld_w2, 16)
                    sp.dma_start(rows2_sb[:, :, :], rows2.partition_broadcast(128)).then_inc(ld_w2, 16)
                    sp.wait_ge(projected, g0 * 2 * NP)
                attention_weights(g0)
                for p in range(NP):
                    pair_weights(g0 * NP + p, p, k == 0 and p == 0)
                cross_weights(g0)
                with sp.Fori(0, NL - 1) as l:
                    g = l + g0
                    ff_weights(g)
                    biases(g)
                    sp.wait_ge(scored[0], (g * 2 + 1) * STEPS)
                    attention_weights(g + 1)
                    cross_weights(g + 1)
                    for p in range(NP):
                        sp.wait_ge(projected, (g * 2 + 1) * NP + p + 1)
                        pair_weights((g + 1) * NP + p, p)
                ff_weights(g0 + NL - 1)
                biases(g0 + NL - 1)
            for b in range(B):
                sp.wait_ge(res_ready[b], 2 + 6 * NL)
                sp.dma_start(out[b:b + 1, :, :].rearrange("b (q p) d -> p (b q) d", p=128),
                             tiles(t, b)).then_inc(stored, 16)
            sp.wait_ge(stored, 32)

        @block.gpsimd
        def _(pool):
            pool.memset(ident[:, :], 0.0).then_inc(const_ready, 1)
            pool.wait_ge(const_ready, 1)
            pool.affine_select(out=ident[:, :], in_=ident[:, :], compare_op=ALU.not_equal, fill=1.0,
                               base=0, pattern=[[-1, 128]], channel_multiplier=1).then_inc(const_ready, 1)
            pool.memset(neghalf[:, :], -0.5).then_inc(const_ready, 1)
            pool.memset(p0[:, :, :], 0.0).then_inc(bd_zero, 1)
            pool.memset(KBD[:, :, :, :, :], 0.0).then_inc(bd_zero, 1)
            pool.memset(VBD[:, :, :, :, :], 0.0).then_inc(bd_zero, 1)

            def norm_factor(e, b, eps):
                pool.wait_ge(ln_mv, e + 1)
                pool.sem_inc(pool_passed, 1)
                pool.tensor_scalar(vpe[:, QT * b:QT * b + QT], tiles(mv, b)[:, :, 1:2].rearrange("p j o -> p (j o)"),
                                   eps, None, ALU.add).then_inc(ln_vpe, 1)
                pool.wait_ge(ln_vpe, e + 1)
                pool.tensor_tensor(rstd[:, QT * b:QT * b + QT], vpe[:, QT * b:QT * b + QT],
                                   neghalf[:, QT * b:QT * b + QT], ALU.pow).then_inc(ln_rstd, 1)

            def low(dst, hi, i, split):
                pool.wait_ge(split_hi, split + 1)
                pool.tensor_tensor(dst, raw[:, i, 0:dst.shape[1]], hi.bitcast(F32),
                                   ALU.subtract).then_inc(split_lo, 1)

            def low_A(p, i, split):
                low(flat(Al[:, p % NP, :, :]), flat(Ah[:, p % NP, :, :]), i, split)

            def low_H(p, h, i, split):
                low(Hl[:, p % 2, h, :], Hh[:, p % 2, h, :], i, split)

            def low_tn(b, g):
                pool.wait_ge(tn_high[b], g + 1)
                pool.tensor_tensor(tnl[:, b, :], tnT[:, b, :], tnh[:, b, :].bitcast(F32),
                                   ALU.subtract).then_inc(tn_low[b], 1)

            def add_bias(e, b, bias):
                pool.wait_ge(ln_xhat, e + 1)
                pool.sem_inc(pool_passed, 1)
                pool.tensor_tensor(tiles(t, b), tiles(t, b),
                                   bias.to_broadcast([128, QT, D]),
                                   ALU.add).then_inc(bias_added[b], 1)

            def half(c):
                rest = c.kind[2]
                for s in range(STEPS):
                    p, q = divmod(s, QT)
                    if q == 0 and before(c, p):
                        pool.wait_ge(rinv_ready, c.pair + p)
                        pool.sem_inc(pool_passed, 1)
                        pool.tensor_copy(rx[:, :, :, :], rinv[:, (p - 1) % 2, :, :].rearrange("p h q -> p q h")
                                         .unsqueeze(3).to_broadcast([128, QT, 2, HD])).then_inc(rx_ready, 1)
                    lows(c, s, 0)
                    lows(c, s, 1)
                    if rest:
                        rest_of_layer(c, s)
                    if c.kind == FIRST and s == STATS1:
                        norm_factor(c.norm - 1, 1, EPS)
                        add_bias(c.norm - 1, 1, first_sb[:, c.k:c.k + 1, :])
                    if c.kind == FIRST and s == SPLIT1:
                        low_tn(1, c.g)
                    lows(c, s, 2)

            def lows(c, s, i):
                name = c.slots.get((s, i), " ")
                if name[0] == "A":
                    low_A(int(name[1]), c.buffer(name), c.split(name))
                if name[0] == "H":
                    low_H(int(name[1]), int(name[2]), c.buffer(name), c.split(name))

            def rest_of_layer(c, s):
                rb, rg, more = c.rb, c.rg, c.kind[3]
                if s == SELF_DONE + STATS:
                    norm_factor(c.norm, rb, EPS)
                if s == SELF_DONE + NORM:
                    pool.wait_ge(ld_rows, (rg + 2) * 16)
                    add_bias(c.norm, rb, rows_sb[:, 0:1, :])
                for j in range(QT):
                    if s == CROSS[j] + CROSS_SUM:
                        pool.wait_ge(x_inv, (rg * 2 + rb) * QT + j + 1)
                        pool.tensor_tensor(XB[:, j, :, :], XB[:, j, :, :],
                                           xinv[:, j, :].unsqueeze(2).to_broadcast([128, H, SK]),
                                           ALU.mult).then_inc(x_norm, 1)
                for j in range(QT):
                    if s == CROSS[j]:
                        pool.wait_ge(x_max, (rg * 2 + rb) * QT + j + 1)
                        pool.tensor_tensor(XB[:, j, :, :], XB[:, j, :, :],
                                           xmax[:, j, :].unsqueeze(2).to_broadcast([128, H, SK]),
                                           ALU.subtract).then_inc(x_sub, 1)
                if s == CROSS_DONE + STATS:
                    norm_factor(c.norm + 1, rb, EPS)
                if s == CROSS_DONE + NORM:
                    add_bias(c.norm + 1, rb, rows_sb[:, 1:2, :])
                if s == FF_DONE + STATS and more:
                    norm_factor(c.norm + 2, rb, EPS)
                if s == FF_DONE + NORM and more:
                    add_bias(c.norm + 2, rb, rows_sb[:, 2:3, :])
                if s == SPLIT0 and more:
                    low_tn(rb, rg + 1)

            pool.wait_ge(ld_rows, 16)
            for k in range(2):
                if k:
                    pool.wait_ge(ff_out, FREE + 2 * NL)
                    pool.memset(v2[:, :, :], 0.0).then_inc(bd_zero, 1)
                    for b in range(B):
                        norm_factor(6 * NL + b, b, EPS2)
                first = Count(k, 0, 0, FIRST).split() - 3
                low_A(0, 0, first)
                norm_factor(k * (2 + 6 * NL), 0, EPS)
                add_bias(k * (2 + 6 * NL), 0, first_sb[:, k:k + 1, :])
                low_tn(0, k * NL)
                for h in range(2):
                    low_H(0, h, (1 + h) % 2, first + 1 + h)
                each_half(pool, k, half)

        @block.vector
        def _(dve):
            n1 = 0

            def stage1(ins):
                nonlocal n1
                n1 += 1
                ins.then_inc(dve1, 1)

            def read_T(dst):
                for b in range(B):
                    stage1(dve.tensor_copy(dst[:, b, :], flat(TR[b][:, :, :])))

            def queries_keys_values(cols_, v_stage):
                for b in range(B):
                    stage1(dve.tensor_scalar(q0T[:, b, :], SC[b][:, :], cols_[:, 0:1], None, ALU.add))
                stage1(dve.tensor_scalar(k0T[:, :], X[:, 0:B * SK], cols_[:, 1:2], None, ALU.add))
                v_stage()

            dve.wait_ge(pe1, 1)
            stage1(dve.tensor_copy(ctxT[:, :], X[0:DK, 0:B * SK]))
            read_T(xT)
            dve.wait_ge(pe1, 2)
            dve.wait_ge(ld_w0, 80)
            queries_keys_values(cols0_sb, lambda: stage1(
                dve.tensor_tensor(v0[:, :], O[0:B * SK, 0:D], rows0_sb[0:B * SK, 0, :], ALU.add)))
            dve.wait_ge(pe1, 3)
            scores0 = X[:, 0:NT * SK].rearrange("p (j m) -> p j m", j=NT)
            stage1(dve.tensor_reduce(m0[:, :], scores0, AX.X, ALU.max))
            dve.wait_ge(dve1, 8)
            stage1(dve.tensor_tensor(s0[:, :, :], scores0,
                                     m0[:, :].unsqueeze(2).to_broadcast([128, NT, SK]), ALU.subtract))
            dve.wait_ge(act1, 1)
            stage1(dve.tensor_reduce(z0[:, :], s0[:, :, :], AX.X, ALU.add))
            dve.wait_ge(dve1, 10)
            stage1(dve.reciprocal(m0[:, :], z0[:, :]))
            dve.wait_ge(dve1, 11)
            dve.wait_ge(bd_zero, 3)
            for b in range(B):
                stage1(dve.tensor_tensor(p0[:, QT * b:QT * b + QT, SK * b:SK * b + SK], tiles(s0, b),
                                         m0[:, QT * b:QT * b + QT].unsqueeze(2).to_broadcast([128, QT, SK]),
                                         ALU.mult))
            dve.wait_ge(pe1, 4)
            for b in range(B):
                stage1(dve.tensor_copy(p0T[:, b, :], flat(TR[b][0:B * SK, :, :])))
            dve.wait_ge(pe1, 5)
            for b in range(B):
                stage1(dve.tensor_copy(a0T[:, b, :], SC[b][:, :]))
            stage1(dve.tensor_tensor(t[:, :, :], t[:, :, :], rows0_sb[:, 1:2, :].to_broadcast([128, NT, D]),
                                     ALU.add))
            dve.wait_ge(dve1, 18)
            dve.wait_ge(pe1, 6)
            for b in range(B):
                dve.tensor_tensor(tiles(t, b), ACC[b][:, :, :], tiles(t, b), ALU.add).then_inc(res_ready[b], 1)
            dve.wait_ge(ld_mask, 32)
            dve.tensor_scalar(cap[:, :, :], cap[:, :, :].bitcast(I32), 0, MASKED, ALU.is_equal, ALU.mult).then_inc(cap_ready, 1)
            dve.tensor_scalar(ccap[:, :, :], cm_sb[:, :, :], 0, MASKED, ALU.is_equal, ALU.mult).then_inc(cap_ready, 1)

            def statistics(e, b, res):
                dve.wait_ge(res_ready[b], res)
                for j in range(QT * b, QT * b + QT):
                    ins = dve.bn_stats(stats[:, j, :], t[:, j, :])
                ins.then_inc(ln_stats, 1)
                dve.wait_ge(ln_stats, e + 1)
                dve.sem_inc(dve_passed, 1)
                for j in range(QT * b, QT * b + QT):
                    ins = dve.bn_aggr(mv[:, j, :], stats[:, j, :])
                ins.then_inc(ln_mv, 1)

            def norm_tiles(e, b):
                dve.wait_ge(ln_rstd, e + 1)
                for j in range(QT * b, QT * b + QT):
                    ins = dve.tensor_scalar(xhat[:, j, :], t[:, j, :], mv[:, j, 0:1], rstd[:, j:j + 1],
                                            ALU.subtract, ALU.mult)
                ins.then_inc(ln_xhat, 1)

            def residual(b, sub):
                dve.wait_ge(bias_added[b], sub + 1)
                dve.tensor_tensor(tiles(t, b), ACC[b][:, :, :], tiles(t, b), ALU.add).then_inc(res_ready[b], 1)

            def product(width, i, split, f, first=False):
                dve.wait_ge(fill, f + 1)
                if not first:
                    dve.wait_ge(split_lo, split - 1)
                    dve.sem_inc(dve_passed, 1)
                dve.tensor_copy(raw[:, i, 0:width], X[:, 0:width]).then_inc(fill_read, 1)

            def half(c):
                carry, own, rest, _ = c.kind
                b, k = c.b, c.k
                for s in range(STEPS):
                    p, q = divmod(s, QT)
                    n = c.step + s
                    if q == 0 and before(c, p):
                        for h in range(2):
                            dve.wait_ge(expd[h], n)
                        dve.reciprocal(rinv[:, (p - 1) % 2, :, :],
                                       rsum[:, (p - 1) % 2, :, :]).then_inc(rinv_ready, 1)
                    for h in range(2 * own):
                        dve.wait_ge(scored[h], n + 1)
                        if carry or s >= 2:
                            dve.wait_ge(expd[h], n - 1)
                        dve.sem_inc(dve_passed, 1)
                        dve.tensor_tensor_reduce(Ms[:, s % 2, h, :], SC[h][:, :], cap[:, b * QT + q, :], -SCALE,
                                                 3.0e38, ALU.add, ALU.min,
                                                 nmax[:, s % 2, h:h + 1]).then_inc(capped[h], 1)
                    slot(c, s, 0)
                    slot(c, s, 1)
                    if q == 1 and before(c, p):
                        dve.wait_ge(pv_done, n - 1)
                        dve.wait_ge(fill_read, FREE + c.fill(f"R{p - 1}") + 1)
                        dve.tensor_tensor(OT[:, :], O[:, :], Rsb[:, :], ALU.mult).then_inc(ot_ready, 1)
                    if (s > 0 and own) or (s == 0 and carry):
                        dve.wait_ge(turned[1], n)
                        if carry or s >= 3:
                            dve.wait_ge(pv_done, n - 2)
                        dve.tensor_copy(PT[:, (s - 1) % 2, 1, :, :], TR[1][:, :, :]).then_inc(pt_ready[1], 1)
                    slot(c, s, 2)
                    if rest:
                        rest_of_layer(c, s)
                    if c.kind == FIRST and s == STATS1:
                        statistics(c.norm - 1, 1, c.g * 3 + 1 + k)
                        norm_tiles(c.norm - 1, 1)

            def slot(c, s, i):
                name = c.slots.get((s, i), " ")
                rb = c.rb
                f = c.fill(name) if name != " " else None
                if name[0] == "A":
                    product(2 * D, c.buffer(name), c.split(name), f)
                if name[0] == "H":
                    product(S, c.buffer(name), c.split(name), f)
                if name[0] == "S":
                    j = int(name[1])
                    dve.wait_ge(fill, f + 1)
                    dve.tensor_tensor(XB[:, j, :, :], X[:, :].rearrange("p (h m) -> p h m", h=H),
                                      ccap[:, rb:rb + 1, :].to_broadcast([128, H, SK]),
                                      ALU.add).then_inc(fill_read, 1)
                    dve.wait_ge(fill_read, FREE + f + 1)
                    dve.tensor_reduce(xmax[:, j, :], XB[:, j, :, :], AX.X, ALU.max).then_inc(x_max, 1)
                if name[0] == "F" and int(name[1]) % 2:
                    m = int(name[1])
                    dve.wait_ge(fill, f + 1)
                    dve.tensor_scalar(hT[:, m, :], X[:, :], cols_sb[:, 2 + m:3 + m], 0.0,
                                      ALU.add, ALU.max).then_inc(fill_read, 1)

            def rest_of_layer(c, s):
                rb, rg, k, more = c.rb, c.rg, c.k, c.kind[3]
                tile = (rg * 2 + rb) * QT
                if s == SELF_DONE:
                    dve.wait_ge(projected, (rg * 2 + rb + 1) * NP)
                    residual(rb, rg * 3)
                if s == SELF_DONE + STATS:
                    statistics(c.norm, rb, rg * 3 + 2 + k)
                if s == SELF_DONE + NORM:
                    norm_tiles(c.norm, rb)
                for j in range(QT):
                    if s == CROSS[j] + CROSS_SUM:
                        dve.wait_ge(x_exp, tile + j + 1)
                        dve.tensor_reduce(xsum[:, j, :], XB[:, j, :, :], AX.X, ALU.add).then_inc(x_sum, 1)
                        dve.wait_ge(x_sum, tile + j + 1)
                        dve.reciprocal(xinv[:, j, :], xsum[:, j, :]).then_inc(x_inv, 1)
                if s == CROSS_DONE:
                    dve.wait_ge(x_out, tile + QT)
                    residual(rb, rg * 3 + 1)
                if s == CROSS_DONE + STATS:
                    statistics(c.norm + 1, rb, rg * 3 + 3 + k)
                if s == CROSS_DONE + NORM:
                    norm_tiles(c.norm + 1, rb)
                if s == FF_DONE:
                    dve.wait_ge(ff_out, FREE + rg * 2 + rb + 1)
                    residual(rb, rg * 3 + 2)
                if s == FF_DONE + STATS and more:
                    statistics(c.norm + 2, rb, rg * 3 + 4 + k)
                if s == FF_DONE + NORM and more:
                    norm_tiles(c.norm + 2, rb)

            for k in range(2):
                g0 = k * NL
                if k:
                    base = n1
                    dve.wait_ge(pe1, 7)
                    read_T(xT)
                    dve.wait_ge(pe1, 8)
                    dve.wait_ge(ld_w2, 64)
                    dve.wait_ge(bd_zero, 4)
                    queries_keys_values(cols2_sb, lambda: [stage1(dve.tensor_tensor(
                        v2[SK * b:SK * b + SK, b, :], O[SK * b:SK * b + SK, 0:D],
                        rows2_sb[SK * b:SK * b + SK, 0, :], ALU.add)) for b in range(B)])
                    dve.wait_ge(pe1, 9)
                    stage1(dve.tensor_reduce(m2[:, :], X[0:B * SK, :], AX.X, ALU.max))
                    dve.wait_ge(dve1, base + 8)
                    stage1(dve.tensor_scalar(m2[:, :], m2[:, :], -SCALE1, None, ALU.mult))
                    dve.wait_ge(act1, 2)
                    stage1(dve.reciprocal(m2[:, :], z2[:, :]))
                    dve.wait_ge(dve1, base + 10)
                    stage1(dve.tensor_scalar(p2[:, :], p2[:, :], m2[:, 0:1], None, ALU.mult))
                    dve.wait_ge(pe1, 10)
                    for b in range(B):
                        stage1(dve.tensor_tensor(tiles(t, b), ACC[b][:, :, :], tiles(t, b), ALU.add))
                    dve.wait_ge(dve1, base + 13)
                    for b in range(B):
                        statistics(6 * NL + b, b, 1 + 3 * NL)
                        norm_tiles(6 * NL + b, b)
                    dve.wait_ge(ln_xhat, 6 * NL + 2)
                    stage1(dve.tensor_tensor(xhat[:, :, :], xhat[:, :, :],
                                             rows2_sb[:, 1:2, :].to_broadcast([128, NT, D]), ALU.mult))
                    dve.wait_ge(dve1, base + 14)
                    for b in range(B):
                        dve.tensor_tensor(tiles(t, b), tiles(xhat, b), rows2_sb[:, 2:3, :].to_broadcast([128, QT, D]),
                                          ALU.add).then_inc(res_ready[b], 1)
                if k == 0:
                    dve.wait_ge(cap_ready, 2)
                at = Count(k, 0, 0, FIRST).entry
                first = Count(k, 0, 0, FIRST).split() - 3
                product(2 * D, 0, first, at + ENTRY.index("A0"), k == 0)
                statistics(k * (2 + 6 * NL), 0, g0 * 3 + 1 + k)
                norm_tiles(k * (2 + 6 * NL), 0)
                for h in range(2):
                    product(S, (1 + h) % 2, first + 1 + h, at + ENTRY.index(f"H0{h}"), k == 0 and h == 0)
                each_half(dve, k, half)

        @block.scalar
        def _(act):
            act.wait_ge(dve1, 9)
            act.activation(s0[:, :, :], s0[:, :, :], ACT.Exp, scale=SCALE1).then_inc(act1, 1)

            def high(dst, src, f):
                act.wait_ge(fill_read, FREE + f + 1)
                act.activation(dst, src, ACT.Copy).then_inc(split_hi, 1)

            def high_A(p, i, f):
                high(flat(Ah[:, p % NP, :, :]), raw[:, i, 0:2 * D], f)

            def high_H(p, h, i, f):
                high(Hh[:, p % 2, h, :], raw[:, i, :], f)

            def normed(b, f, scale, bias):
                act.wait_ge(fill, f + 1)
                act.activation(tnT[:, b, :], X[:, :], ACT.Identity, scale=scale,
                               bias=bias).then_inc(fill_read, 1)

            def normed_high(b, f, k):
                normed(b, f, norm_sb[:, k, 0:1], norm_sb[:, k, 1:2])
                act.wait_ge(fill_read, FREE + f + 1)
                act.activation(tnh[:, b, :], tnT[:, b, :], ACT.Copy).then_inc(tn_high[b], 1)

            def fold_out(name, f):
                act.wait_ge(fill, f + 1)
                if name in "KU":
                    for h in range(2):
                        bd = KBD if name == "K" else VBD
                        ins = act.activation(bd[HD * h:HD * h + HD, :, :, h, :], X[HD * h:HD * h + HD, :]
                                             .rearrange("p (n b m) -> p n b m", n=NP, b=B), ACT.Copy)
                elif name[0] == "M":
                    a = int(name[1])
                    ins = act.activation(Mw[:, :, a * 256:a * 256 + 256].rearrange("p b (n m) -> p n b m", n=4),
                                         X[:, :].rearrange("p (n b m) -> p n b m", n=4, b=B), ACT.Copy)
                else:
                    ins = act.activation(flat(Nw[:, int(name[1]), :, :]), X[:, :], ACT.Copy)
                ins.then_inc(fill_read, 1)

            def half(c):
                carry, own, rest, _ = c.kind
                for s in range(STEPS):
                    p, q = divmod(s, QT)
                    n = c.step + s
                    def exponentials(h):
                        act.wait_ge(capped[h], FREE + n + 1)
                        if carry or s >= 2:
                            act.wait_ge(turned[h], n - 1)
                        act.activation(E[:, s % 2, h, :], Ms[:, s % 2, h, :], ACT.Exp, scale=-1.0,
                                       bias=nmax[:, s % 2, h:h + 1],
                                       accum_out=rsum[:, p % 2, h, q:q + 1]).then_inc(expd[h], 1)

                    slot(c, s, 0)
                    if own:
                        exponentials(0)
                    slot(c, s, 1)
                    if own:
                        exponentials(1)
                    highs(c, s, 0)
                    highs(c, s, 1)
                    if rest:
                        rest_of_layer(c, s)
                    if (s > 0 and own) or (s == 0 and carry):
                        act.wait_ge(turned[0], n)
                        if carry or s >= 3:
                            act.wait_ge(pv_done, n - 2)
                        act.activation(PT[:, (s - 1) % 2, 0, :, :], TR[0][:, :, :], ACT.Copy).then_inc(pt_ready[0], 1)
                    slot(c, s, 2)
                    highs(c, s, 2)

            def highs(c, s, i):
                name = c.slots.get((s, i), " ")
                if name[0] == "A":
                    high_A(int(name[1]), c.buffer(name), c.fill(name))
                if name[0] == "H":
                    high_H(int(name[1]), int(name[2]), c.buffer(name), c.fill(name))

            def slot(c, s, i):
                name = c.slots.get((s, i), " ")
                rb, rg, k = c.rb, c.rg, c.k
                f = c.fill(name) if name != " " else None
                if name[0] == "V":
                    act.wait_ge(fill, f + 1)
                    act.activation(flat(V[:, int(name[1]) % 2, :, :]), X[:, :], ACT.Copy).then_inc(fill_read, 1)
                if name[0] == "R":
                    act.wait_ge(fill, f + 1)
                    act.activation(Rsb[:, :], X[:, :], ACT.Copy).then_inc(fill_read, 1)
                if name == "T1":
                    normed(rb, f, norm_sb[:, k, 0:1], norm_sb[:, k, 1:2])
                if name == "T2":
                    act.wait_ge(ld_ff, (rg + 1) * 32)
                    normed(rb, f, cols_sb[:, 0:1], cols_sb[:, 1:2])
                if name == "T0":
                    normed_high(rb, f, k)
                if name == "E":
                    normed_high(1, f, k)
                if name[0] == "P":
                    j = int(name[1])
                    act.wait_ge(fill, f + 1)
                    if j >= 2:
                        act.wait_ge(x_out, (rg * 2 + rb) * QT + j - 1)
                    act.activation(flat(PX[:, j % 2, :, :]), X[:, :], ACT.Copy).then_inc(fill_read, 1)
                if name[0] == "F" and int(name[1]) % 2 == 0:
                    m = int(name[1])
                    act.wait_ge(fill, f + 1)
                    act.activation(hT[:, m, :], X[:, :], ACT.Relu,
                                   bias=cols_sb[:, 2 + m:3 + m]).then_inc(fill_read, 1)
                if name in FOLD:
                    fold_out(name, f)

            def rest_of_layer(c, s):
                for j in range(QT):
                    if s == CROSS[j] + CROSS_EXP:
                        act.wait_ge(x_sub, (c.rg * 2 + c.rb) * QT + j + 1)
                        act.activation(XB[:, j, :, :], XB[:, j, :, :], ACT.Exp, scale=SCALE).then_inc(x_exp, 1)

            for k in range(2):
                if k:
                    act.wait_ge(dve1, 18 + 9)
                    act.activation(p2[:, :], X[0:B * SK, :], ACT.Exp, scale=SCALE1, bias=m2[:, 0:1],
                                   accum_out=z2[:, 0:1]).then_inc(act1, 1)
                at = Count(k, 0, 0, FIRST).entry
                if k == 0:
                    act.wait_ge(ld_w0, 80)
                for f, name in enumerate(ENTRY):
                    if name == "A0":
                        high_A(0, 0, at + f)
                    elif name == "T":
                        normed_high(0, at + f, k)
                    else:
                        high_H(0, int(name[2]), (1 + int(name[2])) % 2, at + f)
                if k == 0:
                    act.wait_ge(bd_zero, 3)
                each_half(act, k, half)

        @block.tensor
        def _(pe):
            for free in (*capped, *pt_ready, fill_read):
                pe.sem_inc(free, FREE)

            def three(out_, wh, wl, mh, ml):
                pe.matmul(out_, wh, ml, start=True, stop=False)
                pe.matmul(out_, wl, mh, start=False, stop=False)
                return pe.matmul(out_, wh, mh, start=False, stop=True)

            def turn_tokens(src):
                for b in range(B):
                    for q in range(QT):
                        ins = pe.transpose(TR[b][:, q, :], src[:, QT * b + q, :], ident[:, :])
                return ins

            def queries_keys_values(w, wkv):
                for b in range(B):
                    pe.matmul(SC[b][:, :], w[:, 0, :], xT[:, b, :], start=True, stop=True)
                pe.matmul(X[:, 0:B * SK], wkv[:, 0, :], ctxT[:, :], start=True, stop=True)
                return pe.matmul(O[0:B * SK, 0:D], ctxT[:, :], wkv[:, 1, :], start=True, stop=True)

            pe.wait_ge(const_ready, 3)
            pe.wait_ge(ld_in, 32)
            pe.transpose(X[0:DK, 0:B * SK], ctx_sb[:, :], ident[0:B * SK, 0:B * SK])
            turn_tokens(t).then_inc(pe1, 1)
            pe.wait_ge(dve1, 3)
            pe.wait_ge(ld_w0, 80)
            queries_keys_values(w0_sb, w0kv_sb).then_inc(pe1, 1)
            pe.wait_ge(dve1, 7)
            for j in range(NT):
                b, q = divmod(j, QT)
                mm = pe.matmul(X[:, j * SK:j * SK + SK], q0T[:, b, q * 128:q * 128 + 128],
                               k0T[:, b * SK:b * SK + SK], start=True, stop=True)
            mm.then_inc(pe1, 1)
            pe.wait_ge(dve1, 13)
            for j in range(NT):
                b, q = divmod(j, QT)
                mm = pe.transpose(TR[b][0:B * SK, q, :], p0[:, j, :], ident[:, :])
            mm.then_inc(pe1, 1)
            pe.wait_ge(dve1, 15)
            for b in range(B):
                mm = pe.matmul(SC[b][:, :], v0[:, :], p0T[:, b, :], start=True, stop=True)
            mm.then_inc(pe1, 1)
            pe.wait_ge(dve1, 17)
            for j in range(NT):
                b, q = divmod(j, QT)
                mm = pe.matmul(ACC[b][:, q, :], a0T[:, b, q * 128:q * 128 + 128], w0_sb[:, 1, :],
                               start=True, stop=True)
            mm.then_inc(pe1, 1)

            def turn_normed(f, e, b):
                pe.wait_ge(fill_read, FREE + f)
                pe.wait_ge(ln_xhat, e + 1)
                for q in range(QT):
                    ins = pe.transpose(X[:, q * 128:q * 128 + 128], xhat[:, QT * b + q, :], ident[:, :])
                ins.then_inc(fill, 1)

            def fold_qk(g, f, p):
                if p % NP == 0:
                    pe.wait_ge(ld_wqk, (g + 1) * 16)
                pe.wait_ge(fill_read, FREE + f)
                for h in range(2):
                    mm = pe.matmul(X[:, h * D:h * D + D], wqk_sb[:, p % NP, 1, h, :], wqk_sb[:, p % NP, 0, h, :],
                                   start=True, stop=True)
                mm.then_inc(fill, 1)

            def keys(f, b, p, h):
                pe.wait_ge(fill_read, FREE + f)
                three(X[:, :], Ah[:, p % NP, h, :], Al[:, p % NP, h, :], tnh[:, b, :],
                      tnl[:, b, :]).then_inc(fill, 1)

            def fold_context(name, f, g):
                pe.wait_ge(fill_read, FREE + f)
                if name == "K":
                    pe.wait_ge(ld_c, (g + 1) * 32)
                if name in "KU":
                    for n in range(NP):
                        mm = pe.matmul(X[:, n * 64:n * 64 + 64], ckv_sb[:, "KU".index(name), n, :], ctxT[:, :],
                                       start=True, stop=True)
                elif name[0] == "M":
                    for m in range(4):
                        n = int(name[1]) * 4 + m
                        mm = pe.matmul(X[:, m * 128:m * 128 + 128], cqo_sb[:, 0, n, :],
                                       KBD[:, n, :, :, :].rearrange("p b h m -> p (b h m)"), start=True, stop=True)
                else:
                    for n in range(NP):
                        mm = pe.matmul(X[64 * (n % 2):64 * (n % 2) + 64, (n // 2) * D:(n // 2) * D + D],
                                       VBD[:, n, int(name[1]), :, :].rearrange("p h m -> p (h m)"),
                                       cqo_sb[:, 1, n, :], start=True, stop=True)
                mm.then_inc(fill, 1)

            def half(c):
                carry, own, rest, _ = c.kind
                g, b = c.g, c.b
                for s in range(STEPS):
                    p, q = divmod(s, QT)
                    n = c.step + s
                    for h in range(2 * own):
                        pe.wait_ge(capped[h], FREE + n)
                        if s == 0:
                            pe.wait_ge(tn_low[b], g + 1)
                        if q == 0:
                            pe.wait_ge(split_lo, c.split(f"H{p}{h}") + 1 if p else c.split() - 1 + h)
                        three(SC[h][:, :], tnh[:, b, q * 128:q * 128 + 128], tnl[:, b, q * 128:q * 128 + 128],
                              Hh[:, p % 2, h, :], Hl[:, p % 2, h, :]).then_inc(scored[h], 1)
                    slot(c, s, 0)
                    if q == 2 and before(c, p):
                        pb = b if p > 0 else 1 - b
                        lp = (p - 1) % NP
                        pe.wait_ge(ot_ready, c.pair + p)
                        for m in range(QT):
                            mm = pe.matmul(ACC[pb][:, m, :], OT[:, m * 128:m * 128 + 128], wvo_sb[:, lp, 1, :],
                                           start=(lp == 0 and m == 0), stop=(lp == NP - 1), skip_group_check=True)
                        mm.then_inc(projected, 1)
                    if (own and s >= 2) or (carry and s < 2):
                        times_v(c, s)
                    if rest:
                        rest_of_layer(c, s)
                    slot(c, s, 1)
                    if (s > 0 and own) or (s == 0 and carry):
                        for h in range(2):
                            pe.wait_ge(expd[h], n)
                            pe.wait_ge(pt_ready[h], FREE + n - 1)
                            for m in range(KT):
                                mm = pe.transpose(TR[h][:, m, :], E[:, (s - 1) % 2, h, m * 128:m * 128 + 128],
                                                  ident[:, :])
                            mm.then_inc(turned[h], 1)
                    slot(c, s, 2)

            def slot(c, s, i):
                name = c.slots.get((s, i), " ")
                if name == " ":
                    return
                f = c.fill(name)
                rb, rg, b, g = c.rb, c.rg, c.b, c.g
                p = s // QT
                if name[0] == "V":
                    pe.wait_ge(ld_wvo, (g * NP + p + 1) * 16)
                    pe.wait_ge(fill_read, FREE + f)
                    for m in range(KT):
                        mm = pe.matmul(X[:, m * 128:m * 128 + 128], tnT[:, b, m * 128:m * 128 + 128],
                                       wvo_sb[:, p, 0, :], start=True, stop=True)
                    mm.then_inc(fill, 1)
                if name[0] == "A":
                    fold_qk(g + b, f, p + 1)
                if name[0] == "H":
                    nb = b if p < NP - 1 else 1 - b
                    if p == NP - 1:
                        pe.wait_ge(tn_low[nb], g + b + 1)
                    if f"A{p + 1}" in c.order:
                        pe.wait_ge(split_lo, c.split(f"A{p + 1}") + 1)
                    keys(f, nb, p + 1, int(name[2]))
                if name[0] == "R":
                    pe.wait_ge(rx_ready, c.pair + p)
                    pe.wait_ge(fill_read, FREE + f)
                    for m in range(QT):
                        mm = pe.transpose(X[:, m * 128:m * 128 + 128],
                                          rx[:, m, :, :].rearrange("p h d -> p (h d)"), ident[:, :])
                    mm.then_inc(fill, 1)
                if name == "E":
                    turn_normed(f, c.norm - 1, 1)
                if name[0] == "T":
                    turn_normed(f, c.norm + {"T1": 0, "T2": 1, "T0": 2}[name], rb)
                if name[0] == "S":
                    j = int(name[1])
                    pe.wait_ge(fill_read, FREE + f)
                    pe.matmul(X[:, :], tnT[:, rb, j * 128:j * 128 + 128], Mw[:, rb, :], start=True,
                              stop=True).then_inc(fill, 1)
                if name[0] == "P":
                    j = int(name[1])
                    pe.wait_ge(x_norm, (rg * 2 + rb) * QT + j + 1)
                    pe.wait_ge(fill_read, FREE + f)
                    xb = XB[:, j, :, :].rearrange("p h m -> p (h m)")
                    for m in range(4):
                        mm = pe.transpose(X[:, m * 128:m * 128 + 128], xb[:, m * 128:m * 128 + 128], ident[:, :])
                    mm.then_inc(fill, 1)
                if name[0] == "F":
                    m = int(name[1])
                    if m == 0:
                        pe.wait_ge(ld_ff, (rg + 1) * 32)
                    pe.wait_ge(fill_read, FREE + f)
                    pe.matmul(X[:, :], ffw_sb[:, 0, m * 128:m * 128 + 128], tnT[:, rb, :], start=True,
                              stop=True).then_inc(fill, 1)
                if name in FOLD:
                    fold_context(name, f, g)

            def times_v(c, s):
                n = c.step + s - 2
                p, q = divmod(s - 2, QT)
                if q == 0 and (p > 0 or c.kind[0]):
                    pe.wait_ge(ot_ready, c.pair + p)
                for h in range(2):
                    pe.wait_ge(pt_ready[h], FREE + n + 1)
                for m in range(KT):
                    for h in range(2):
                        mm = pe.matmul(O[HD * h:HD * h + HD, q * 128:q * 128 + 128],
                                       V[:, p % 2, m, HD * h:HD * h + HD], PT[:, s % 2, h, m, :],
                                       start=(m == 0), stop=(m == KT - 1))
                mm.then_inc(pv_done, 1)

            def rest_of_layer(c, s):
                rb = c.rb
                for j in range(QT):
                    if s == CROSS_OUT[j]:
                        pe.wait_ge(fill_read, FREE + c.fill(f"P{j}") + 1)
                        for m in range(4):
                            mm = pe.matmul(ACC[rb][:, j, :], PX[:, j % 2, m, :], Nw[:, rb, m, :],
                                           start=(m == 0), stop=(m == 3))
                        mm.then_inc(x_out, 1)
                if s == FF_OUT:
                    pe.wait_ge(fill_read, FREE + c.fill(f"F{NF - 1}") + 1)
                if 0 <= s - FF_OUT < 2:
                    for q in range(2 * (s - FF_OUT), 2 * (s - FF_OUT) + 2):
                        for m in range(NF):
                            mm = pe.matmul(ACC[rb][:, q, :], hT[:, m, q * 128:q * 128 + 128],
                                           ffw_sb[:, 1, m * 128:m * 128 + 128], start=(m == 0), stop=(m == NF - 1))
                    if s == FF_OUT + 1:
                        mm.then_inc(ff_out, 1)

            for k in range(2):
                if k:
                    d1 = 18
                    for b in range(B):
                        pe.wait_ge(res_ready[b], 1 + 3 * NL)
                    pe.wait_ge(ld_w2, 64)
                    turn_tokens(t).then_inc(pe1, 1)
                    pe.wait_ge(dve1, d1 + 2)
                    queries_keys_values(w2_sb, w2kv_sb).then_inc(pe1, 1)
                    pe.wait_ge(dve1, d1 + 7)
                    for b in range(B):
                        mm = pe.matmul(X[SK * b:SK * b + SK, :], k0T[:, SK * b:SK * b + SK], q0T[:, b, :],
                                       start=True, stop=True)
                    mm.then_inc(pe1, 1)
                    pe.wait_ge(dve1, d1 + 11)
                    for j in range(NT):
                        b, q = divmod(j, QT)
                        mm = pe.matmul(ACC[b][:, q, :], p2[:, q * 128:q * 128 + 128], v2[:, b, :],
                                       start=True, stop=True)
                    mm.then_inc(pe1, 1)
                g0 = k * NL
                at = Count(k, 0, 0, FIRST).entry
                for f, name in enumerate(ENTRY):
                    if name == "A0":
                        fold_qk(g0, at + f, 0)
                    elif name == "T":
                        turn_normed(at + f, k * (2 + 6 * NL), 0)
                    else:
                        if name == "H00":
                            pe.wait_ge(tn_low[0], g0 + 1)
                            pe.wait_ge(split_lo, Count(k, 0, 0, FIRST).split() - 2)
                        keys(at + f, 0, 0, int(name[2]))
                each_half(pe, k, half)


def kernel(**inputs):
    import numpy as np
    import concourse.bacc as bacc
    from concourse.bass_utils import run_bass_kernel_spmd

    a = {k: np.asarray(v) for k, v in inputs.items()}
    stacks = ("L1_xattn_", "L3_xattn_")

    def both(name):
        return np.concatenate([a[s + name] for s in stacks])

    G = 2 * NL
    wqT = both("sa_q").transpose(0, 2, 1).reshape(G, NP, 2, HD, D)
    wkT = both("sa_kv")[:, :, :H * HD].transpose(0, 2, 1).reshape(G, NP, 2, HD, D)
    wv = both("sa_kv")[:, :, H * HD:].reshape(G, D, NP, 128).transpose(0, 2, 1, 3).reshape(G * NP, D, 128)
    wo = both("sa_ow").reshape(G * NP, 128, D)
    cqT = both("ca_q").transpose(0, 2, 1).reshape(G, NP, 128, D)
    co = both("ca_ow").reshape(G, NP, 128, D)
    w2f = both("ff_w2").reshape(G, NF, 128, D).transpose(0, 2, 1, 3).reshape(G, 128, NF * D)
    arrays = {
        "x": a["x"], "ctx": a["ctx_512"], "mask": a["mask_BxSxS_ik0"], "cmask": a["mask_Bx1xS2_if1"],
        "w0": np.stack([a["L0_xattn_Wq"], a["L0_xattn_Wo"]], 1),
        "w0kv": np.stack([a["L0_xattn_Wk"], a["L0_xattn_Wv"]], 1),
        "w2": a["L2_xattn_Wq"][:, None, :],
        "w2kv": np.stack([a["L2_xattn_Wk"], a["L2_xattn_Wv"]], 1),
        "rows0": np.stack([a["L0_xattn_bv"], a["L0_xattn_bo"]]),
        "rows2": np.stack([a["L2_xattn_bv"], a["L2_xattn_gamma"], a["L2_xattn_beta"]]),
        "cols0": np.stack([a["L0_xattn_bq"], a["L0_xattn_bk"]], 1),
        "cols2": np.stack([a["L2_xattn_bq"], a["L2_xattn_bk"]], 1),
        "wqk": np.stack([wqT, wkT], 2).transpose(0, 4, 1, 2, 3, 5), "wvo": np.stack([wv, wo], 2),
        "ckv": both("ca_kv").reshape(G, DK, 2, NP, 128),
        "cqo": np.stack([cqT, co], 1).transpose(0, 3, 1, 2, 4),
        "ffw": np.stack([both("ff_w1"), w2f], 2),
        "cols": np.concatenate([both("pre_g")[:, :, None], both("pre_b")[:, :, None],
                                both("ff_b1").reshape(G, NF, 128).transpose(0, 2, 1)], 2),
        "first": both("sa_ob")[::NL],
        "rows": np.stack([both("ca_ob"), both("ff_b2"), np.roll(both("sa_ob"), -1, 0)], 1),
        "norms": np.stack([np.stack([a[s + "norm_g"], a[s + "norm_b"]], 1) for s in stacks], 1),
    }
    arrays = {k: np.ascontiguousarray(v) for k, v in arrays.items()}
    nc = bacc.Bacc("TRN2", target_bir_lowering=False, num_devices=1)
    aps = {k: nc.dram_tensor(k, v.shape, mybir.dt.from_np(v.dtype), kind="ExternalInput").ap()
           for k, v in arrays.items()}
    out = nc.dram_tensor("out", (B, S, D), F32, kind="ExternalOutput").ap()
    build(nc, out=out, **aps)
    r = run_bass_kernel_spmd(nc, [arrays], core_ids=[0])
    return r.results[0]["out"]
```
